# Optimizing a Trainium2 kernel written in Bass

```python
import numpy as np
import jax
import jax.numpy as jnp

def _softmax(x, axis=-1):
    return jax.nn.softmax(x, axis=axis)

def _gelu(x):
    return jax.nn.gelu(x, approximate=True)

def _silu(x):
    return jax.nn.silu(x)

def _sigmoid(x):
    return jax.nn.sigmoid(x)

def _layernorm(x, axis=-1, eps=1e-05):
    m = jnp.mean(x, axis=axis, keepdims=True)
    v = jnp.var(x, axis=axis, keepdims=True)
    return (x - m) / jnp.sqrt(v + eps)

def _scatter_add(tgt, idx, src, axis=0):
    return tgt.at[idx].add(src)

def _segment_sum(src, seg, n):
    return jax.ops.segment_sum(src, seg, n)
kernel_name = 'mk_flamingo_gated_d1_seqx_r8_395466'

def setup_inputs(seed: int=0):
    np.random.seed(seed)
    _w = jnp.asarray

    def _rec_inputs():
        import jax
        import jax.numpy as jnp
        _rk = jax.random.key(seed)
        x = 7.22e-05 + 1 * jax.random.normal(jax.random.fold_in(_rk, 1), (8, 256, 128), jnp.float32)
        _lenS = 256 - jax.random.randint(jax.random.fold_in(_rk, 7), (8,), 0, max(1, 256 // 4) + 1, jnp.int32)
        _lenS2 = 1601 - jax.random.randint(jax.random.fold_in(_rk, 8), (8,), 0, max(1, 1601 // 4) + 1, jnp.int32)
        _ctx_1024P = jax.random.normal(jax.random.fold_in(_rk, 11), (8, 16, 128), jnp.float32)
        _ctx_1024c = jax.random.dirichlet(jax.random.fold_in(_rk, 511), 0.3 * jnp.ones((16,), jnp.float32), (8, 1601))
        _ctx_1024t = jnp.einsum('bsk,bkd->bsd', _ctx_1024c, _ctx_1024P)
        _ctx_1024t = _ctx_1024t * jax.lax.rsqrt(jnp.mean(jnp.square(_ctx_1024t)) + 1e-12) * 0.953939
        ctx_1024 = 4.13588e-05 + 0.999923 * (_ctx_1024t + 0.3 * jax.random.normal(jax.random.fold_in(_rk, 611), (8, 1601, 128), jnp.float32))
        _g = jax.random.normal(jax.random.fold_in(_rk, 9001), (2, 1), jnp.float32)
        _g = jnp.sign(_g) * jnp.maximum(jnp.abs(_g), 1.0) + (_g == 0) * 1.0
        g_xattn = _g[0]
        g_ffn = _g[1]
        return (x, ctx_1024, g_xattn, g_ffn)
    x, ctx_1024, g_xattn, g_ffn = _rec_inputs()

    def _L0_xattn_setup():
        import jax, jax.numpy as jnp
        import numpy as np
        B, L, S, D, H = (4, 256, 256, 128, 16)
        E = D // H
        key = jax.random.key(seed)
        ks = jax.random.split(key, 7)
        sc = 1.0 / np.sqrt(D)
        return {'q': jax.random.normal(ks[0], (B, L, D), dtype=jnp.float32), 'k': jax.random.normal(ks[1], (B, S, D), dtype=jnp.float32), 'v': jax.random.normal(ks[2], (B, S, D), dtype=jnp.float32), 'Wq': jax.random.normal(ks[3], (D, D), dtype=jnp.float32) * sc, 'bq': jnp.zeros((D,), dtype=jnp.float32), 'Wo': jax.random.normal(ks[4], (D, D), dtype=jnp.float32) * sc, 'bo': jnp.zeros((D,), dtype=jnp.float32)}
    _L0_xattn_all = _L0_xattn_setup()
    _L0_xattn_in = {k: v for k, v in _L0_xattn_all.items() if k in ('Wq', 'bq', 'Wo', 'bo')}
    del _L0_xattn_all

    def _L0_ffn_setup():
        import jax, jax.numpy as jnp
        import numpy as np
        H = 128
        I = 64
        E = 64
        G = 8
        TOPK_GROUP = 4
        K = 8
        I_SH = 128
        SCALE = 2.5

        def _route(x, router_w, e_bias):
            T = x.shape[0]
            scores = jax.nn.sigmoid(x.astype(jnp.float32) @ router_w.T.astype(jnp.float32))
            sfc = jax.lax.stop_gradient(scores) + e_bias[None, :]
            group_scores = jax.lax.top_k(sfc.reshape(T, G, E // G), 2)[0].sum(-1)
            _, gidx = jax.lax.top_k(group_scores, TOPK_GROUP)
            gmask = jax.nn.one_hot(gidx, G, dtype=sfc.dtype).sum(1)
            smask = jnp.repeat(gmask, E // G, axis=1)
            masked = jnp.where(smask > 0, sfc, 0.0)
            _, topk_idx = jax.lax.top_k(masked, K)
            w = jnp.take_along_axis(scores, topk_idx, axis=1)
            w = w / (w.sum(-1, keepdims=True) + 1e-20)
            return (topk_idx, w * SCALE)
        key = jax.random.key(seed)
        ks = jax.random.split(key, 9)
        s = 0.02
        return {'hidden_states': jax.random.normal(ks[0], (2, 128, H), jnp.float32), 'router_w': jax.random.normal(ks[1], (E, H), jnp.float32) * s, 'e_bias': jnp.zeros((E,), jnp.float32), 'Wg': jax.random.normal(ks[2], (E, H, I), jnp.float32) * s, 'Wu': jax.random.normal(ks[3], (E, H, I), jnp.float32) * s, 'Wd': jax.random.normal(ks[4], (E, I, H), jnp.float32) * s, 'SWg': jax.random.normal(ks[5], (H, I_SH), jnp.float32) * s, 'SWu': jax.random.normal(ks[6], (H, I_SH), jnp.float32) * s, 'SWd': jax.random.normal(ks[7], (I_SH, H), jnp.float32) * s}
    _L0_ffn_all = _L0_ffn_setup()
    _L0_ffn_in = {k: v for k, v in _L0_ffn_all.items() if k in ('router_w', 'e_bias', 'Wg', 'Wu', 'Wd', 'SWg', 'SWu', 'SWd')}
    del _L0_ffn_all
    return {'x': x, 'ctx_1024': ctx_1024, 'g_xattn': g_xattn, 'g_ffn': g_ffn, 'L0_xattn_Wq': _L0_xattn_in['Wq'], 'L0_xattn_bq': _L0_xattn_in['bq'], 'L0_xattn_Wo': _L0_xattn_in['Wo'], 'L0_xattn_bo': _L0_xattn_in['bo'], 'L0_ffn_router_w': _L0_ffn_in['router_w'], 'L0_ffn_e_bias': _L0_ffn_in['e_bias'], 'L0_ffn_Wg': _L0_ffn_in['Wg'], 'L0_ffn_Wu': _L0_ffn_in['Wu'], 'L0_ffn_Wd': _L0_ffn_in['Wd'], 'L0_ffn_SWg': _L0_ffn_in['SWg'], 'L0_ffn_SWu': _L0_ffn_in['SWu'], 'L0_ffn_SWd': _L0_ffn_in['SWd']}

def reference(x, ctx_1024, g_xattn, g_ffn, L0_xattn_Wq, L0_xattn_bq, L0_xattn_Wo, L0_xattn_bo, L0_ffn_router_w, L0_ffn_e_bias, L0_ffn_Wg, L0_ffn_Wu, L0_ffn_Wd, L0_ffn_SWg, L0_ffn_SWu, L0_ffn_SWd):
    import jax
    import jax.numpy as jnp

    def _L0_xattn_ref(q, k, v, Wq, bq, Wo, bo):
        import jax, jax.numpy as jnp
        import numpy as np
        B, L, S, D, H = (4, 256, 256, 128, 16)
        E = D // H
        b, l, _ = q.shape
        s = k.shape[1]
        qp = (q @ Wq.T + bq).reshape(b, l, H, E)
        kp = (k @ Wq.T + bq).reshape(b, s, H, E)
        vp = (v @ Wq.T + bq).reshape(b, s, H, E)
        scale = 1.0 / np.sqrt(E)
        scores = jnp.einsum('blhe,bshe->bhls', qp, kp)
        attn = jax.nn.softmax(scale * scores, axis=-1)
        out = jnp.einsum('bhls,bshd->blhd', attn, vp)
        out = jnp.transpose(out, (0, 2, 1, 3)).reshape(b, l, H * E)
        return out @ Wo.T + bo

    def _L0_ffn_ref(hidden_states, router_w, e_bias, Wg, Wu, Wd, SWg, SWu, SWd):
        import jax, jax.numpy as jnp
        import numpy as np
        H = 128
        I = 64
        E = 64
        G = 8
        TOPK_GROUP = 4
        K = 8
        I_SH = 128
        SCALE = 2.5

        def _route(x, router_w, e_bias):
            T = x.shape[0]
            scores = jax.nn.sigmoid(x.astype(jnp.float32) @ router_w.T.astype(jnp.float32))
            sfc = jax.lax.stop_gradient(scores) + e_bias[None, :]
            group_scores = jax.lax.top_k(sfc.reshape(T, G, E // G), 2)[0].sum(-1)
            _, gidx = jax.lax.top_k(group_scores, TOPK_GROUP)
            gmask = jax.nn.one_hot(gidx, G, dtype=sfc.dtype).sum(1)
            smask = jnp.repeat(gmask, E // G, axis=1)
            masked = jnp.where(smask > 0, sfc, 0.0)
            _, topk_idx = jax.lax.top_k(masked, K)
            w = jnp.take_along_axis(scores, topk_idx, axis=1)
            w = w / (w.sum(-1, keepdims=True) + 1e-20)
            return (topk_idx, w * SCALE)
        orig_shape = hidden_states.shape
        x = hidden_states.reshape(-1, orig_shape[-1])
        T = x.shape[0]
        topk_idx, topk_w = _route(x, router_w, e_bias)
        coef = jnp.zeros((T, E), topk_w.dtype).at[jnp.arange(T)[:, None], topk_idx].add(topk_w)
        g = jnp.einsum('th,ehi->tei', x, Wg)
        u = jnp.einsum('th,ehi->tei', x, Wu)
        h = jax.nn.silu(g) * u * coef[:, :, None]
        moe_out = jnp.einsum('tei,eih->th', h, Wd)
        shared = jax.nn.silu(x @ SWg) * (x @ SWu) @ SWd
        return (moe_out + shared).reshape(orig_shape)
    x = x + jnp.tanh(g_xattn[0]) * _L0_xattn_ref(_layernorm(x, axis=-1), ctx_1024, ctx_1024, L0_xattn_Wq, L0_xattn_bq, L0_xattn_Wo, L0_xattn_bo)
    x = x + jnp.tanh(g_ffn[0]) * _L0_ffn_ref(_layernorm(x, axis=-1), L0_ffn_router_w, L0_ffn_e_bias, L0_ffn_Wg, L0_ffn_Wu, L0_ffn_Wd, L0_ffn_SWg, L0_ffn_SWu, L0_ffn_SWd)
    return x

_drawn_inputs = setup_inputs


def setup_inputs(seed=0):
    import zlib

    import numpy as np

    out = dict(_drawn_inputs(seed))
    spreads = {'L0_xattn_bq': (0.0, 0.1), 'L0_xattn_bo': (0.0, 0.1), 'L0_ffn_e_bias': (0.0, 0.8)}
    factors = {'L0_ffn_router_w': 8.0,
     'L0_ffn_Wg': 8.0,
     'L0_ffn_Wu': 8.0,
     'L0_ffn_Wd': 8.0,
     'L0_ffn_SWg': 8.0,
     'L0_ffn_SWu': 8.0,
     'L0_ffn_SWd': 8.0}
    for name, (base, spread) in spreads.items():
        noise = np.random.default_rng([zlib.crc32(name.encode()), seed]).standard_normal(out[name].shape)
        drawn = base * np.exp(spread * noise) if base else spread * noise
        out[name] = jnp.asarray(drawn.astype(out[name].dtype))
    for name, factor in factors.items():
        out[name] = (out[name] * factor).astype(out[name].dtype)
    return out
```

```python
from contextlib import ExitStack

import concourse.bass as bass
from concourse import mybir

F32 = mybir.dt.float32
F32R = mybir.dt.float32r
BF16 = mybir.dt.bfloat16
ALU = mybir.AluOpType
ACT = mybir.ActivationFunctionType
AX = mybir.AxisListType

P = 128
HEADS, E = 16, 8
QUAD = 4
EPS = 1e-5
ROUTE_SCALE = 2.5
TOPK_GROUP, TOPK, GROUPS = 4, 8, 8
PICKED = -3.0e38
FILLER = -1.0e38

SLOTS = [(0, 0, 0), (8, 0, 1), (16, 0, 2), (24, 1, 0), (40, 1, 1), (48, 2, 0)]
SHIFT_ROW, SHIFT_ROWS = 32, 2
SLOTS4 = 4
PROBS = 4


def build(nc, x, ctx, g_x, g_f, Wq, bq, Wo, bo, router_w, e_bias, Wg, Wu, Wd, SWg, SWu, SWd, out):
    B, L, D = x.shape
    S = ctx.shape[1]
    NE, _, I = Wg.shape
    T = B * L // P
    ST = -(-S // P)
    LAST = S - (ST - 1) * P
    CH = 4 * P
    SC = -(-S // CH)
    SPAD = ST * P
    NQ = B * HEADS // QUAD
    QPB = HEADS // QUAD
    SCALE = float(E) ** -0.5
    assert D == P and HEADS * E == P and L == 2 * P and QPB == SLOTS4 and ST % 2 == 1

    k_parts = nc.dram_tensor("k_parts", [3, B, P, SPAD], BF16).ap()
    q_parts = nc.dram_tensor("q_parts", [3, P, B * L], BF16).ap()

    with ExitStack() as top:
        def sb(name, shape, dt=F32, where=top):
            return where.enter_context(nc.sbuf_tensor(name, shape, dt))

        def sem(name):
            return top.enter_context(nc.semaphore(name))

        ps = top.enter_context(nc.psum_tensor("ps", [P, 8, CH], F32))
        ident = sb("ident", [P, P])
        x_sb = sb("x_sb", [P, T, D])
        wqT = sb("wqT", [P, P])
        woT = sb("woT", [P, P])
        rwT = sb("rwT", [P, NE])
        bo_b = sb("bo_b", [P, P])
        eb_b = sb("eb_b", [P, NE])
        gates = sb("gates", [P, 2])
        tanh_g = sb("tanh_g", [P, 2])
        stats = sb("stats", [P, T, 6])
        moments = sb("moments", [P, T, 2])
        rstd = sb("rstd", [P, T])
        o_sb = sb("o_sb", [P, NQ, L])

        v = dict(locals())
        with ExitStack() as held:
            v["v_sb"] = sb("v_sb", [P, B, ST, P], where=held)
            project(nc, v)
            attend(nc, v)
        mix_and_experts(nc, v)


def project(nc, v):
    top, sem = v["top"], v["sem"]
    ps, ident, x_sb, wqT, woT, rwT = v["ps"], v["ident"], v["x_sb"], v["wqT"], v["woT"], v["rwT"]
    stats, moments, rstd = v["stats"], v["moments"], v["rstd"]
    B, L, D, S, T, ST, LAST, CH, SC = (v[n] for n in ("B", "L", "D", "S", "T", "ST", "LAST", "CH", "SC"))
    k_parts, q_parts, NE = v["k_parts"], v["q_parts"], v["NE"]

    v_sb = v["v_sb"]
    with ExitStack() as local:
        def sb(name, shape, dt=F32):
            return local.enter_context(nc.sbuf_tensor(name, shape, dt))

        w_raw = sb("w_raw", [P, 3, P])
        bq_col = sb("bq_col", [P, 1])
        bq_b = sb("bq_b", [P, P])
        xn = sb("xn", [P, T, D])
        raw = sb("raw", [P, 4, 4, D])
        turned = sb("turned", [P, 2, CH])
        full = sb("full", [P, 2, CH])
        rest = sb("rest", [P, 2, CH])
        parts = sb("parts", [P, 2, 3, CH], BF16)

        loaded_small, loaded_x = sem("loaded_small"), sem("loaded_x")
        loaded_ctx = [sem(f"loaded_ctx{i}") for i in range(4)]
        parts_out = [sem(f"parts_out{i}") for i in range(2)]
        ident_made, ident_ready = sem("ident_made"), sem("ident_ready")
        w_turned, w_ready = sem("w_turned"), sem("w_ready")
        stat_done, mean_done, var_ready, std_ready, rstd_ready, xn_ready = (
            sem(n) for n in ("stat_done", "mean_done", "var_ready", "std_ready", "rstd_ready", "xn_ready"))
        chunk_turned, chunk_ready = sem("chunk_turned"), sem("chunk_ready")
        k_done, k_saved, v_done, v_saved = sem("k_done"), sem("k_saved"), sem("v_done"), sem("v_saved")
        part1, rest1, part2, part3 = sem("part1"), sem("rest1"), sem("part2"), sem("part3")
        tanh_done = v["tanh_done"] = sem("tanh_done")

        chunks = [("k", b, c) for b in range(B) for c in range(SC)]
        chunks += [("q", 0, c) for c in range(B * L // CH)]

        def tiles(kind, c):
            if kind == "q":
                return [(i, P) for i in range(4)]
            return [(t - 4 * c, LAST if t == ST - 1 else P) for t in range(4 * c, min(4 * c + 4, ST))]

        def width(kind, c):
            return sum(r for _, r in tiles(kind, c))

        ctx_count = {}
        seen = [0] * 4
        for n, (kind, b, c) in enumerate(chunks):
            if kind == "k":
                full_rows = sum(1 for _, r in tiles(kind, c) if r == P)
                partial = any(r < P for _, r in tiles(kind, c))
                seen[n % 4] += 16 * ((full_rows > 0) + partial)
                ctx_count[n] = seen[n % 4]

        with nc.Block() as block:
            @block.sync
            def _(sp):
                for i, w in enumerate((v["Wq"], v["Wo"])):
                    sp.dma_start(w_raw[:, i, :], w).then_inc(loaded_small, 16)
                sp.dma_start(w_raw[0:NE, 2, :], v["router_w"]).then_inc(loaded_small, 16)
                sp.dma_start(bq_col[:, :], v["bq"].rearrange("(p a) -> p a", a=1)).then_inc(loaded_small, 16)
                row = lambda a: a.rearrange("(a n) -> a n", a=1)
                sp.dma_start(bq_b[:, :], row(v["bq"]).to_broadcast((P, P))).then_inc(loaded_small, 16)
                sp.dma_start(v["bo_b"][:, :], row(v["bo"]).to_broadcast((P, P))).then_inc(loaded_small, 16)
                sp.dma_start(v["eb_b"][:, :], row(v["e_bias"]).to_broadcast((P, NE))).then_inc(loaded_small, 16)
                sp.dma_start(v["gates"][:, 0:1], row(v["g_x"]).to_broadcast((P, 1))).then_inc(loaded_small, 16)
                sp.dma_start(v["gates"][:, 1:2], row(v["g_f"]).to_broadcast((P, 1))).then_inc(loaded_small, 16)
                for n, (kind, b, c) in enumerate(chunks):
                    if kind == "q":
                        break
                    if n == 4:
                        sp.dma_start(x_sb[:, :, :], v["x"].rearrange("b (t p) d -> p (b t) d", p=P))\
                          .then_inc(loaded_x, 16)
                    if n >= 4:
                        sp.wait_ge(chunk_turned, n - 3)
                    whole = sum(1 for _, r in tiles(kind, c) if r == P)
                    first = c * CH
                    if whole:
                        sp.dma_start(raw[:, n % 4, 0:whole, :],
                                     v["ctx"][b, first:first + whole * P, :].rearrange("(t p) d -> p t d", p=P))\
                          .then_inc(loaded_ctx[n % 4], 16)
                    if whole < len(tiles(kind, c)):
                        sp.dma_start(raw[0:LAST, n % 4, whole, :], v["ctx"][b, first + whole * P:S, :])\
                          .then_inc(loaded_ctx[n % 4], 16)

            @block.gpsimd
            def _(pool):
                nc.gpsimd.memset(ident[:, :], 0.0).then_inc(ident_made, 1)
                pool.wait_ge(ident_made, 1)
                nc.gpsimd.affine_select(out=ident[:, :], in_=ident[:, :], compare_op=ALU.not_equal, fill=1.0,
                                        base=0, pattern=[[-1, P]], channel_multiplier=1).then_inc(ident_ready, 1)
                for n, (kind, b, c) in enumerate(chunks):
                    w, s = width(kind, c), n % 2
                    pool.wait_ge(part1, n + 1)
                    nc.gpsimd.tensor_tensor(rest[:, s, 0:w], full[:, s, 0:w], parts[:, s, 0, 0:w], ALU.subtract)\
                      .then_inc(rest1, 1)
                    pool.wait_ge(part2, n + 1)
                    nc.gpsimd.tensor_tensor(parts[:, s, 2, 0:w], rest[:, s, 0:w], parts[:, s, 1, 0:w], ALU.subtract)\
                      .then_inc(part3, 1)
                    pool.wait_ge(part3, n + 1)
                    if kind == "k":
                        to = k_parts[:, b, :, c * CH:c * CH + w]
                    else:
                        to = q_parts[:, :, c * CH:c * CH + w]
                    pool.dma_start(to.rearrange("t p s -> p t s"), parts[:, s, :, 0:w]).then_inc(parts_out[s], 16)
                for s in range(2):
                    pool.wait_ge(parts_out[s], 16 * len(range(s, len(chunks), 2)))

            @block.tensor
            def _(pe):
                pe.wait_ge(ident_ready, 1)
                pe.wait_ge(loaded_small, 9 * 16)
                for i, n in enumerate((P, P, NE)):
                    last = nc.tensor.transpose(ps[:, 7, i * P:i * P + n], w_raw[0:n, i, :], ident[0:n, 0:n])
                last.then_inc(w_turned, 1)
                pe.wait_ge(w_ready, 1)

                def turn(n):
                    kind, b, c = chunks[n]
                    if kind == "k":
                        pe.wait_ge(loaded_ctx[n % 4], ctx_count[n])
                    else:
                        pe.wait_ge(xn_ready, T)
                    if n >= 2:
                        pe.wait_ge(chunk_ready, n - 1)
                    for i, r in tiles(kind, c):
                        src = raw[0:r, n % 4, i, :] if kind == "k" else xn[:, 4 * c + i, :]
                        last = nc.tensor.transpose(ps[:, n % 2, i * P:i * P + r], src, ident[0:r, 0:r])
                    last.then_inc(chunk_turned, 1)

                turn(0)
                values = 0
                for n, (kind, b, c) in enumerate(chunks):
                    if n + 1 < len(chunks):
                        turn(n + 1)
                    pe.wait_ge(chunk_ready, n + 1)
                    if n >= 2:
                        pe.wait_ge(k_saved, n - 1)
                    w = width(kind, c)
                    nc.tensor.matmul(ps[:, 2 + n % 2, 0:w], wqT[:, :], turned[:, n % 2, 0:w], start=True, stop=True)\
                      .then_inc(k_done, 1)
                    if kind == "k":
                        if values >= 2:
                            pe.wait_ge(v_saved, values - 1)
                        for i, r in tiles(kind, c):
                            last = nc.tensor.matmul(ps[0:r, 4 + n % 2, i * P:(i + 1) * P],
                                                    turned[:, n % 2, i * P:i * P + r], wqT[:, :], start=True, stop=True)
                        last.then_inc(v_done, 1)
                        values += 1

            @block.scalar
            def _(act):
                act.wait_ge(w_turned, 1)
                for i, (dst, n) in enumerate(((wqT, P), (woT, P), (rwT, NE))):
                    last = nc.scalar.activation(dst[:, :], ps[:, 7, i * P:i * P + n], ACT.Copy)
                last.then_inc(w_ready, 1)

                def copy_turned(n):
                    w = width(chunks[n][0], chunks[n][2])
                    act.wait_ge(chunk_turned, n + 1)
                    if n >= 2:
                        act.wait_ge(k_done, n - 1)
                        vals = sum(1 for ch in chunks[:n - 1] if ch[0] == "k")
                        act.wait_ge(v_done, vals)
                    nc.scalar.activation(turned[:, n % 2, 0:w], ps[:, n % 2, 0:w], ACT.Copy).then_inc(chunk_ready, 1)

                copy_turned(0)
                for n, (kind, b, c) in enumerate(chunks):
                    w, s = width(kind, c), n % 2
                    if n == 8:
                        act.wait_ge(var_ready, 1)
                        nc.scalar.activation(rstd[:, :], rstd[:, :], ACT.Sqrt).then_inc(std_ready, 1)
                    if n + 1 < len(chunks):
                        copy_turned(n + 1)
                    act.wait_ge(k_saved, n + 1)
                    if n >= 2:
                        act.wait_ge(parts_out[s], 16 * (n // 2))
                    nc.scalar.activation(parts[:, s, 0, 0:w], full[:, s, 0:w], ACT.Copy).then_inc(part1, 1)
                    act.wait_ge(rest1, n + 1)
                    nc.scalar.activation(parts[:, s, 1, 0:w], rest[:, s, 0:w], ACT.Copy).then_inc(part2, 1)
                nc.scalar.activation(v["tanh_g"][:, :], v["gates"][:, :], ACT.Tanh).then_inc(tanh_done, 1)

            @block.vector
            def _(dve):
                dve.wait_ge(loaded_small, 9 * 16)
                values = 0
                for n, (kind, b, c) in enumerate(chunks):
                    w, s = width(kind, c), n % 2
                    if n == 4:
                        dve.wait_ge(loaded_x, 16)
                        for t in range(T):
                            nc.vector.bn_stats(stats[:, t, :], x_sb[:, t, :]).then_inc(stat_done, 1)
                        for t in range(T):
                            dve.wait_ge(stat_done, t + 1)
                            nc.vector.bn_aggr(moments[:, t, :], stats[:, t, :]).then_inc(mean_done, 1)
                        dve.wait_ge(mean_done, T)
                        nc.vector.tensor_scalar(rstd[:, :], moments[:, :, 1], EPS, None, ALU.add).then_inc(var_ready, 1)
                    if n == 12:
                        dve.wait_ge(std_ready, 1)
                        nc.vector.reciprocal(rstd[:, :], rstd[:, :]).then_inc(rstd_ready, 1)
                        dve.wait_ge(rstd_ready, 1)
                        for t in range(T):
                            nc.vector.tensor_scalar(xn[:, t, :], x_sb[:, t, :], moments[:, t, 0:1], rstd[:, t:t + 1],
                                                    ALU.subtract, ALU.mult).then_inc(xn_ready, 1)
                    dve.wait_ge(k_done, n + 1)
                    if n >= 2:
                        dve.wait_ge(rest1, n - 1)
                    nc.vector.tensor_scalar(full[:, s, 0:w], ps[:, 2 + s, 0:w], bq_col[:, 0:1], None, ALU.add)\
                      .then_inc(k_saved, 1)
                    if kind == "k":
                        values += 1
                        dve.wait_ge(v_done, values)
                        whole = sum(1 for _, r in tiles(kind, c) if r == P)
                        if whole:
                            bias = bq_b[:, :].rearrange("p (a n) -> p a n", a=1).to_broadcast((P, whole, P))
                            last = nc.vector.tensor_tensor(
                                v_sb[:, b, 4 * c:4 * c + whole, :],
                                ps[:, 4 + s, 0:whole * P].rearrange("p (t n) -> p t n", n=P), bias, ALU.add)
                        if whole < len(tiles(kind, c)):
                            last = nc.vector.tensor_tensor(v_sb[0:LAST, b, ST - 1, :],
                                                           ps[0:LAST, 4 + s, whole * P:(whole + 1) * P],
                                                           bq_b[0:LAST, :], ALU.add)
                        last.then_inc(v_saved, 1)


def attend(nc, v):
    sem, ps, ident, o_sb, v_sb = v["sem"], v["ps"], v["ident"], v["o_sb"], v["v_sb"]
    B, L, S, ST, LAST, CH, SC, NQ, SCALE = (v[n] for n in ("B", "L", "S", "ST", "LAST", "CH", "SC", "NQ", "SCALE"))
    k_parts, q_parts, SPAD = v["k_parts"], v["q_parts"], v["SPAD"]
    LT = L // P
    MAXES = QUAD * LT * SC
    BM, NM, BO = 4, 3, 7
    TURN_AT = 3
    TURN_CHUNKS = MAXES * (TURN_AT + 1) // ST
    BT = BM + TURN_CHUNKS % NM
    LATE = [max(m for m in range(MAXES) if m % NM == k) + NM - MAXES for k in range(NM)]
    LOADS = 2 * 2 * len(SLOTS) * 16

    with ExitStack() as local:
        def sb(name, shape, dt=F32):
            return local.enter_context(nc.sbuf_tensor(name, shape, dt))

        kst = sb("kst", [P, SLOTS4, 2, SPAD], BF16)
        qst = sb("qst", [P, SLOTS4, 2, 2 * L], BF16)
        probs = sb("probs", [P, PROBS, 2, 2 * L])
        vq = sb("vq", [P, 2, ST, QUAD, E + 1])
        mx = sb("mx", [P, LT * QUAD, SC])
        negm = sb("negm", [P, LT * QUAD])
        negm1 = sb("negm1", [P, LT * QUAD], BF16)
        MP = 64 + SHIFT_ROW + SHIFT_ROWS
        mpad = sb("mpad", [P, LT, 2, P])

        zeroed, ones_set, quad_loaded = sem("zeroed"), sem("ones_set"), [sem(f"quad_loaded{s}") for s in range(SLOTS4)]
        max_scored, max_free = sem("max_scored"), sem("max_free")
        max_taken, max_split, max_first = sem("max_taken"), sem("max_split"), sem("max_first")
        negmax_ready, negmax_turned, shift_placed = sem("negmax_ready"), sem("negmax_turned"), sem("shift_placed")
        shift_cleared, v_placed, v_settled = sem("shift_cleared"), sem("v_placed"), sem("v_settled")
        scores_ready, probs_ready, probs_free, out_free = (
            sem("scores_ready"), sem("probs_ready"), sem("probs_free"), sem("out_free"))

        def rows(t):
            return LAST if t == ST - 1 else P

        def chunk_list(t):
            return range(MAXES * t // ST, MAXES * (t + 1) // ST)

        with nc.Block() as block:
            @block.sync
            def _(sp):
                def load(b, i):
                    for base, kp, qp in SLOTS:
                        for j in range(2):
                            r = 64 * j + base
                            kd = k_parts[kp, b if isinstance(b, int) else bass.ds(b, 1), :, 0:S]
                            if not isinstance(b, int):
                                kd = kd.rearrange("a p s -> (a p) s")
                            kd = kd.rearrange("(h e) s -> e h s", e=E)[:, QUAD * i + j:QUAD * i + j + 3:2, :]
                            sp.dma_start(kst[r:r + E, i, :, 0:S], kd).then_inc(quad_loaded[i], 16)
                            at = b * L
                            qd = q_parts[qp, :, at:at + L] if isinstance(b, int) else q_parts[qp, :, bass.ds(at, L)]
                            qd = qd.rearrange("(h e) l -> e h l", e=E)[:, QUAD * i + j:QUAD * i + j + 3:2, :]
                            sp.dma_start(qst[r:r + E, i, :, j * L:(j + 1) * L], qd).then_inc(quad_loaded[i], 16)

                sp.wait_ge(ones_set, 2)
                for i in range(SLOTS4):
                    load(0, i)
                with sp.Fori(1, B) as b:
                    for i in range(SLOTS4):
                        sp.wait_ge(out_free, SLOTS4 * b + i - 1)
                        load(b, i)

            @block.gpsimd
            def _(pool):
                nc.gpsimd.memset(kst[:, :, :, :], 0.0).then_inc(zeroed, 1)
                nc.gpsimd.memset(vq[:, :, :, :, :], 1.0).then_inc(zeroed, 1)
                pool.wait_ge(zeroed, 3)
                for j in range(2):
                    r = 64 * j + SHIFT_ROW
                    nc.gpsimd.memset(kst[r:r + SHIFT_ROWS, :, :, :], 1.0).then_inc(ones_set, 1)
                pool.wait_ge(ones_set, 2)
                with pool.Fori(0, B) as b:
                    for i in range(SLOTS4):
                        q = SLOTS4 * b + i
                        pool.wait_ge(out_free, q + 1)
                        src = v_sb[:, bass.ds(b, 1), :, QUAD * E * i:QUAD * E * (i + 1)]\
                            .rearrange("p a t (g e) -> p (a t) g e", e=E)
                        nc.gpsimd.tensor_copy(vq[:, i % 2, 0:ST - 1, :, 0:E], src[:, 0:ST - 1, :, :])
                        nc.gpsimd.tensor_copy(vq[0:LAST, i % 2, ST - 1, :, 0:E], src[0:LAST, ST - 1, :, :])\
                          .then_inc(v_placed, 1)
                        pool.wait_ge(v_placed, q + 1)
                        pool.sem_inc(v_settled, 1)
                        for j in range(2):
                            r = 64 * j + SHIFT_ROW
                            nc.gpsimd.memset(qst[r:r + SHIFT_ROWS, (i + 2) % SLOTS4, :, :], 0.0)\
                              .then_inc(shift_cleared, 1)
                        pool.wait_ge(shift_cleared, 2 * q + 2)

            @block.tensor
            def _(pe):
                def max_chunk(b, i, k):
                    c, g, lt = k % SC, (k // SC) % QUAD, k // (SC * QUAD)
                    p, j = g // 2, g % 2
                    w = min(CH, S - c * CH)
                    done = MAXES * (SLOTS4 * b + i) + k
                    if k == TURN_CHUNKS and not (isinstance(b, int) and b == 0 and i == 0):
                        pe.wait_ge(shift_placed, 2 * (SLOTS4 * b + i - 1) + 2)
                    pe.wait_ge(max_free, done + 1 if k >= NM else done - k + 1 + LATE[k])
                    nc.tensor.matmul(ps[:, BM + k % NM, 0:w],
                                     qst[:, i, p, j * L + lt * P:j * L + (lt + 1) * P],
                                     kst[:, i, p, c * CH:c * CH + w], start=True, stop=True).then_inc(max_scored, 1)

                def turn_maxima(q, next_follows=True):
                    pe.wait_ge(negmax_ready, q + 1)
                    if next_follows:
                        pe.wait_ge(max_free, MAXES * (q + 1) + TURN_CHUNKS + 1)
                    for p in range(2):
                        for lt in range(LT):
                            last = nc.tensor.transpose(ps[:, BT, p * L + lt * P:p * L + (lt + 1) * P],
                                                       mpad[:, lt, p, :], ident[:, :])
                    last.then_inc(negmax_turned, 1)

                def score(b, i, t, between):
                    n = ST * (SLOTS4 * b + i) + t
                    s = (i + t) % 2
                    if t == 0:
                        pe.wait_ge(shift_placed, 2 * (SLOTS4 * b + i) + 2)
                    if not (isinstance(n, int) and n < 2):
                        pe.wait_ge(probs_ready, n - 1)
                    m = rows(t)
                    for p in range(2):
                        last = nc.tensor.matmul(ps[0:m, 2 * s + p, :], kst[:, i, p, t * P:t * P + m],
                                                qst[:, i, p, :], start=True, stop=True)
                        if p == 0:
                            between()
                    last.then_inc(scores_ready, 1)

                def weigh(b, i, t, between):
                    q = SLOTS4 * b + i
                    n = ST * q + t
                    if t == 0:
                        pe.wait_ge(v_placed, q + 1)
                        pe.wait_ge(out_free, q + 2)
                    pe.wait_ge(probs_ready, n + 1)
                    m = rows(t)
                    for g in range(QUAD):
                        p, j = g // 2, g % 2
                        last = nc.tensor.matmul(ps[32 * g:32 * g + E + 1, BO, 0:L],
                                                vq[0:m, i % 2, t, g, :],
                                                probs[0:m, (i * ST + t) % PROBS, p, j * L:(j + 1) * L],
                                                start=(t == 0), stop=(t == ST - 1))
                        if g < QUAD - 1:
                            between(g)
                    last.then_inc(probs_free, 1)

                def batch(b, last_batch):
                    for i in range(SLOTS4):
                        for t in range(ST):
                            bm, im = (b, i + 2) if i + 2 < SLOTS4 else (b + 1, i + 2 - SLOTS4)
                            maxima = not (last_batch and i + 2 >= SLOTS4)
                            if maxima and t == 0:
                                pe.wait_ge(quad_loaded[im], LOADS * (bm + 1))
                                pe.wait_ge(shift_cleared, 2 * (SLOTS4 * b + i) + 2)
                            ks = iter(chunk_list(t) if maxima else ())

                            def next_chunk():
                                for k in ks:
                                    max_chunk(bm, im, k)
                                    break

                            i2, t2 = (i, t + 2) if t + 2 < ST else (i + 1, t + 2 - ST)
                            if i2 < SLOTS4:
                                score(b, i2, t2, lambda: None)
                            elif not last_batch:
                                score(b + 1, 0, t2, lambda: None)
                            next_chunk()
                            weigh(b, i, t, lambda g: next_chunk() if g in (0, 2) else None)
                            for k in ks:
                                max_chunk(bm, im, k)
                            if t == TURN_AT and not (last_batch and i + 1 >= SLOTS4):
                                turn_maxima(SLOTS4 * b + i + 1, not (last_batch and i + 2 >= SLOTS4))

                pe.sem_inc(max_free, NM)
                pe.sem_inc(probs_free, PROBS)
                for i in range(2):
                    pe.wait_ge(quad_loaded[i], LOADS)
                    for k in range(MAXES):
                        if i == 1 and k == TURN_CHUNKS:
                            turn_maxima(0)
                        max_chunk(0, i, k)
                score(0, 0, 0, lambda: None)
                score(0, 0, 1, lambda: None)
                with pe.Fori(0, B - 1) as b:
                    batch(b, False)
                batch(B - 1, True)

            @block.scalar
            def _(act):
                with act.Fori(0, B) as b:
                    for i in range(SLOTS4):
                        for t in range(ST):
                            n = ST * (SLOTS4 * b + i) + t
                            m, s = rows(t), (i + t) % 2
                            act.wait_ge(scores_ready, n + 1)
                            act.wait_ge(probs_free, n + 1)
                            nc.scalar.activation(probs[0:m, (i * ST + t) % PROBS, :, :], ps[0:m, 2 * s:2 * s + 2, :],
                                                 ACT.Exp, scale=SCALE).then_inc(probs_ready, 1)

            @block.vector
            def _(dve):
                nc.vector.memset(qst[:, :, :, :], 0.0).then_inc(zeroed, 1)
                nc.vector.memset(mpad[:, :, :, :], 0.0).then_inc(max_split, 1)
                nc.vector.memset(ps[:, BO, :], 0.0).then_inc(out_free, 2)
                maxpad = mpad[:, :, :, :].rearrange("m l p (j c) -> m (l p) j c", j=2)

                def take(b, i, k):
                    w = min(CH, S - (k % SC) * CH)
                    done = MAXES * (SLOTS4 * b + i) + k
                    dve.wait_ge(max_scored, done + 1)
                    nc.vector.reduce_max(mx[:, k // SC, k % SC:k % SC + 1], ps[:, BM + k % NM, 0:w], AX.X)\
                       .then_inc(max_free, 1)

                def negate(q):
                    dve.wait_ge(max_free, NM + MAXES * (q + 1))
                    if not (isinstance(q, int) and q < 1):
                        dve.wait_ge(negmax_turned, q)
                    nc.vector.tensor_reduce(negm[:, :], mx[:, :, :], AX.X, ALU.max, negate=True).then_inc(max_taken, 1)
                    dve.wait_ge(max_taken, q + 1)
                    nc.vector.tensor_copy(negm1[:, :], negm[:, :]).then_inc(max_first, 1)
                    dve.wait_ge(max_first, q + 1)
                    one = negm1[:, :].rearrange("m (a j) -> m a j", j=2)
                    both = negm[:, :].rearrange("m (a j) -> m a j", j=2)
                    nc.vector.tensor_copy(maxpad[:, :, :, SHIFT_ROW], one).then_inc(max_split, 1)
                    dve.wait_ge(max_split, q + 2)
                    nc.vector.tensor_tensor(maxpad[:, :, :, SHIFT_ROW + 1], both, one, ALU.subtract)\
                       .then_inc(negmax_ready, 1)

                def place(q, i):
                    dve.wait_ge(negmax_turned, q + 1)
                    for j in range(2):
                        r = 64 * j + SHIFT_ROW
                        nc.vector.tensor_copy(qst[r:r + SHIFT_ROWS, i, :, j * L:(j + 1) * L],
                                              ps[r:r + SHIFT_ROWS, BT, :].rearrange("r (p l) -> r p l", p=2))\
                           .then_inc(shift_placed, 1)

                def save(q):
                    dve.wait_ge(probs_free, PROBS + ST * (q + 1))
                    dst = o_sb[:, q:q + 1, :] if isinstance(q, int) else o_sb[:, bass.ds(q, 1), :]
                    nc.vector.tensor_copy(dst.rearrange("p a l -> p (a l)"), ps[:, BO, 0:L])\
                       .then_inc(out_free, 1)

                def batch(b, last_batch):
                    for i in range(SLOTS4):
                        q = SLOTS4 * b + i
                        maxima = not (last_batch and i + 2 >= SLOTS4)
                        bm, im = (b, i + 2) if i + 2 < SLOTS4 else (b + 1, i + 2 - SLOTS4)
                        for k in range(MAXES):
                            if k == TURN_CHUNKS:
                                if not (last_batch and i + 1 >= SLOTS4):
                                    place(q + 1, (i + 1) % SLOTS4)
                            if maxima:
                                take(bm, im, k)
                        save(q)
                        if maxima:
                            negate(SLOTS4 * bm + im)

                for k in range(MAXES):
                    take(0, 0, k)
                negate(0)
                for k in range(MAXES):
                    if k == TURN_CHUNKS:
                        place(0, 0)
                    take(0, 1, k)
                negate(1)
                with dve.Fori(0, B - 1) as b:
                    batch(b, False)
                batch(B - 1, True)


def mix_and_experts(nc, v):
    sem, ps, ident, o_sb, x_sb = v["sem"], v["ps"], v["ident"], v["o_sb"], v["x_sb"]
    B, L, D, T, CH, NE, I, QPB = (v[n] for n in ("B", "L", "D", "T", "CH", "NE", "I", "QPB"))
    stats, moments, rstd, tanh_g = v["stats"], v["moments"], v["rstd"], v["tanh_g"]
    woT, rwT, bo_b, eb_b = v["woT"], v["rwT"], v["bo_b"], v["eb_b"]
    LT = L // P
    UNITS = NE * I // P
    ALLU = UNITS + 1
    NC = B * L // CH
    GROUP = NE // GROUPS
    STAGE = 8

    with ExitStack() as local:
        def sb(name, shape, dt=F32):
            return local.enter_context(nc.sbuf_tensor(name, shape, dt))

        den = sb("den", [P, 2, HEADS])
        attn = sb("attn", [P, 2, QUAD, P])
        attnT = sb("attnT", [P, 2, P])
        proj = sb("proj", [P, 2, P])
        room = o_sb[:, :, :].rearrange("p q l -> p (q l)")
        xn = room[:, 0:T * D].rearrange("p (t d) -> p t d", d=D)
        xnT = room[:, T * D:2 * T * D]
        xr = sb("xr", [P, 2, B * L], F32R)
        wd_sb = sb("wd_sb", [P, ALLU, D])
        wgu = [sb(n, [P, 2, ALLU, P], F32R) for n in ("wg_sb", "wu_sb")]
        stage = sb("stage", [P, 2, CH])
        sel0 = sb("sel0", [P, 4, P])
        sel = sb("sel", [P, UNITS, P], F32R)
        scores = sb("scores", [P, T, NE])
        sfc = sb("sfc", [P, T, NE])
        best = room[:, 2 * T * D:2 * T * D + T * GROUPS * 8].rearrange("p (t g k) -> p t g k", g=GROUPS, k=8)
        gscore = sb("gscore", [P, T, 2 * GROUPS])
        gbest = sb("gbest", [P, T, 8])
        gtake = sb("gtake", [P, T, 8])
        gleft = sb("gleft", [P, T, 2 * GROUPS])
        wsum = sb("wsum", [P, T])
        coef = sb("coef", [P, 2, NE])
        cr = sb("cr", [P, 2, 2, NE])
        crr = sb("crr", [P, 2, NE], F32R)
        coefT = sb("coefT", [P, B * L], F32R)
        gact = sb("gact", [P, 2, CH])
        gu = sb("gu", [P, 2, CH])
        h = sb("h", [P, 2, CH])
        y_sb = sb("y_sb", [P, CH])
        res = sb("res", [P, CH])

        turned_o, den_done, attn_ready, attn_turned, attnT_ready, projected = (
            sem(n) for n in ("turned_o", "den_done", "attn_ready", "attn_turned", "attnT_ready", "projected"))
        biased, mixed, stat2, mean2, var2, std2, rstd2, xn2_ready = (
            sem(n) for n in ("biased", "mixed", "stat2", "mean2", "var2", "std2", "rstd2", "xn2_ready"))
        xn_turned, xnT_ready, logits_ready, scores_done, xr_hi, xr_ready = (
            sem(n) for n in ("xn_turned", "xnT_ready", "logits_ready", "scores_done", "xr_hi", "xr_ready"))
        w_loaded = [sem(f"w_loaded{s}") for s in range(2)]
        wd_loaded, w_cut_hi, w_cut, sel_zero, sel_made, sel_ready = (
            sem(n) for n in ("wd_loaded", "w_cut_hi", "w_cut", "sel_zero", "sel_made", "sel_ready"))
        route, coef_ready, coef_turned, coefT_ready = (
            sem(n) for n in ("route", "coef_ready", "coef_turned", "coefT_ready"))
        g_done, act_done, u_done, gu_done, h_done, unit_free = (
            sem(n) for n in ("g_done", "act_done", "u_done", "gu_done", "h_done", "unit_free"))
        down_done, y_done, y_saved, y_turned, res_ready = (
            sem(n) for n in ("down_done", "y_done", "y_saved", "y_turned", "res_ready"))
        out_sent, x_loaded = sem("out_sent"), sem("x_loaded")

        queries = o_sb[:, :, :].rearrange("p q (a m) -> p q a m", m=P // E)
        folded = lambda a: a.rearrange("(c two) (i g a) d -> c (two i) g a d", two=2, g=QUAD, a=P // E)

        stages = []
        for which, (W, SW) in enumerate(((v["Wg"], v["SWg"]), (v["Wu"], v["SWu"]))):
            for u in range(0, UNITS, 4):
                stages.append((which, u, 4, W[2 * u:2 * u + 8, :, :].rearrange("e h i -> h e i")))
            stages.append((which, UNITS, 1, SW))

        with nc.Block() as block:
            @block.sync
            def _(sp):
                for c in range(NC):
                    for g in range(QUAD):
                        sp.dma_start(x_sb[:, 4 * c + g, :], folded(v["x"])[c, :, g, :, :]).then_inc(x_loaded, 16)
                for n, (_, _, k, src) in enumerate(stages):
                    if n >= 2:
                        sp.wait_ge(w_cut, n - 1)
                    dst = stage[:, n % 2, 0:k * P]
                    if k > 1:
                        dst = dst.rearrange("h (e i) -> h e i", i=I)
                    sp.dma_start(dst, src).then_inc(w_loaded[n % 2], 16)

            @block.gpsimd
            def _(pool):
                pool.dma_start(wd_sb[:, 0:UNITS, :], v["Wd"].rearrange("(u a) i h -> (a i) u h", a=2))\
                    .then_inc(wd_loaded, 16)
                pool.dma_start(wd_sb[:, UNITS, :], v["SWd"]).then_inc(wd_loaded, 16)
                for n in range(UNITS // 4):
                    if n >= 1:
                        pool.wait_ge(sel_ready, n)
                    nc.gpsimd.memset(sel0[:, :, :], 0.0).then_inc(sel_zero, 1)
                    pool.wait_ge(sel_zero, n + 1)
                    for half in range(2):
                        rows = sel0[half * NE:(half + 1) * NE, :, :]
                        last = nc.gpsimd.affine_select(
                            out=rows.rearrange("e u (a i) -> e u a i", a=2), in_=rows.rearrange("e u (a i) -> e u a i", a=2),
                            compare_op=ALU.not_equal, fill=1.0, base=-8 * n,
                            pattern=[[-2, 4], [-1, 2], [0, I]], channel_multiplier=1)
                    last.then_inc(sel_made, 1)
                pool.wait_ge(wd_loaded, 32)

            @block.tensor
            def _(pe):
                for t in range(T):
                    if t >= 2:
                        pe.wait_ge(attn_ready, t - 1)
                    for n in range(4):
                        m = t % 4 * 4 + n
                        last = nc.tensor.transpose(
                            ps[:, t % 2, n * P:(n + 1) * P],
                            queries[:, 8 * (t // 4):8 * (t // 4) + 8, :, m], ident[:, :])
                    last.then_inc(turned_o, 1)
                    if t % 4 == 3 and t > 4:
                        for u in range(t - 7, t - 3):
                            mix_turn(nc, pe, u, ps, attn, ident, attn_ready, attnT_ready, attn_turned)
                            if u >= 1:
                                mix_project(nc, pe, u - 1, ps, attnT, woT, attnT_ready, biased, projected)
                for u in range(T - 4, T):
                    mix_turn(nc, pe, u, ps, attn, ident, attn_ready, attnT_ready, attn_turned)
                    mix_project(nc, pe, u - 1, ps, attnT, woT, attnT_ready, biased, projected)
                mix_project(nc, pe, T - 1, ps, attnT, woT, attnT_ready, biased, projected)
                for c in range(NC):
                    pe.wait_ge(xn2_ready, 4 * c + 4)
                    if c >= 2:
                        pe.wait_ge(xnT_ready, c - 1)
                    for i in range(4):
                        last = nc.tensor.transpose(ps[:, c % 2, i * P:(i + 1) * P], xn[:, 4 * c + i, :], ident[:, :])
                    last.then_inc(xn_turned, 1)
                    if c >= 1:
                        router(nc, pe, c - 1, ps, xnT, rwT, NE, xnT_ready, logits_ready)
                router(nc, pe, NC - 1, ps, xnT, rwT, NE, xnT_ready, logits_ready)
                for t in range(T):
                    pe.wait_ge(coef_ready, t + 1)
                    if t >= 2:
                        pe.wait_ge(coefT_ready, t - 1)
                    nc.tensor.transpose(ps[:, t % 2, 0:P], cr[:, t % 2, :, :].rearrange("p a e -> p (a e)"), ident[:, :])\
                      .then_inc(coef_turned, 1)

            @block.scalar
            def _(act):
                for t in range(T):
                    act.wait_ge(attn_turned, t + 1)
                    if t >= 2:
                        act.wait_ge(projected, t - 1)
                    nc.scalar.activation(attnT[:, t % 2, :], ps[:, 2 + t % 2, 0:P], ACT.Copy).then_inc(attnT_ready, 1)
                act.wait_ge(var2, 1)
                nc.scalar.activation(rstd[:, :], rstd[:, :], ACT.Sqrt).then_inc(std2, 1)
                for c in range(NC):
                    act.wait_ge(xn_turned, c + 1)
                    nc.scalar.activation(xnT[:, c * CH:(c + 1) * CH], ps[:, c % 2, :], ACT.Copy).then_inc(xnT_ready, 1)
                for c in range(T * NE // CH):
                    act.wait_ge(logits_ready, (c + 1) * (CH // NE) // 4)
                    k = CH // NE
                    nc.scalar.activation(scores[:, k * c:k * (c + 1), :],
                                         ps[:, 6 + c, :].rearrange("p (t e) -> p t e", e=NE), ACT.Sigmoid)\
                      .then_inc(scores_done, 1)
                for t in range(T):
                    act.wait_ge(coef_turned, t + 1)
                    nc.scalar.activation(coefT[:, t * P:(t + 1) * P], ps[:, t % 2, 0:P], ACT.Copy)\
                      .then_inc(coefT_ready, 1)

            @block.vector
            def _(dve):
                cuts = iter(range(len(stages)))

                def cut_weights():
                    n = next(cuts, None)
                    if n is None:
                        return
                    which, u, k, _ = stages[n]
                    dve.wait_ge(w_loaded[n % 2], 16 * (n // 2 + 1))
                    hi = wgu[which][:, 0, u:u + k, :].rearrange("h u c -> h (u c)")
                    lo = wgu[which][:, 1, u:u + k, :].rearrange("h u c -> h (u c)")
                    nc.vector.tensor_copy(hi, stage[:, n % 2, 0:k * P]).then_inc(w_cut_hi, 1)
                    dve.wait_ge(w_cut_hi, n + 1)
                    nc.vector.tensor_tensor(lo, stage[:, n % 2, 0:k * P], hi.bitcast(F32), ALU.subtract)\
                       .then_inc(w_cut, 1)

                dve.wait_ge(v["tanh_done"], 1)
                dve.wait_ge(x_loaded, 16 * T)
                for t in range(T):
                    o = ps[:, t % 2, :].rearrange("p (h c) -> p h c", c=32)
                    dve.wait_ge(turned_o, t + 1)
                    nc.vector.reciprocal(den[:, t % 2, :], o[:, :, E]).then_inc(den_done, 1)
                    dve.wait_ge(den_done, t + 1)
                    if t >= 8 and t % 4 == 0:
                        dve.wait_ge(attn_turned, t - 4)
                    d3 = den[:, t % 2, :].rearrange("p (h a) -> p h a", a=1).to_broadcast((P, HEADS, E))
                    at = attn[:, t // 4 % 2, :, t % 4 * 32:(t % 4 + 1) * 32].rearrange("p g (m e) -> p m g e", e=E)
                    nc.vector.tensor_tensor(at, o[:, :, 0:E].rearrange("p (m g) e -> p m g e", g=QUAD),
                                            d3.rearrange("p (m g) e -> p m g e", g=QUAD), ALU.mult)\
                       .then_inc(attn_ready, 1)
                    cut_weights()
                    if t % 4 == 3 and t > 4:
                        for u in range(max(t - 8, 0), t - 4):
                            finish_mix(nc, dve, u, v, ps, proj, projected, biased, mixed)
                for u in range(T - 5, T):
                    finish_mix(nc, dve, u, v, ps, proj, projected, biased, mixed)
                for t in range(T):
                    dve.wait_ge(mixed, t + 1)
                    nc.vector.bn_stats(stats[:, t, :], x_sb[:, t, :]).then_inc(stat2, 1)
                for t in range(T):
                    dve.wait_ge(stat2, t + 1)
                    nc.vector.bn_aggr(moments[:, t, :], stats[:, t, :]).then_inc(mean2, 1)
                dve.wait_ge(mean2, T)
                nc.vector.tensor_scalar(rstd[:, :], moments[:, :, 1], EPS, None, ALU.add).then_inc(var2, 1)
                dve.wait_ge(std2, 1)
                nc.vector.reciprocal(rstd[:, :], rstd[:, :]).then_inc(rstd2, 1)
                dve.wait_ge(rstd2, 1)
                for t in range(T):
                    nc.vector.tensor_scalar(xn[:, t, :], x_sb[:, t, :], moments[:, t, 0:1], rstd[:, t:t + 1],
                                            ALU.subtract, ALU.mult).then_inc(xn2_ready, 1)
                for _ in range(len(stages) - T):
                    cut_weights()
                for n in range(UNITS // 4):
                    dve.wait_ge(sel_made, n + 1)
                    nc.vector.tensor_copy(sel[:, 4 * n:4 * n + 4, :], sel0[:, :, :]).then_inc(sel_ready, 1)
                for c in range(NC):
                    dve.wait_ge(xnT_ready, c + 1)
                    part = slice(c * CH, (c + 1) * CH)
                    nc.vector.tensor_copy(xr[:, 0, part], xnT[:, part]).then_inc(xr_hi, 1)
                    dve.wait_ge(xr_hi, c + 1)
                    nc.vector.tensor_tensor(xr[:, 1, part], xnT[:, part], xr[:, 0, part].bitcast(F32), ALU.subtract)\
                       .then_inc(xr_ready, 1)

                steps = [0]

                def link(ins):
                    steps[0] += 1
                    ins.then_inc(route, 1)

                def settle():
                    dve.wait_ge(route, steps[0])

                dve.wait_ge(scores_done, T * NE // CH)
                ebias = eb_b[:, :].rearrange("p (a e) -> p a e", a=1).to_broadcast((P, T, NE))
                link(nc.vector.tensor_tensor(sfc[:, :, :], scores[:, :, :], ebias, ALU.add))
                link(nc.vector.memset(gscore[:, :, :], FILLER))
                link(nc.vector.memset(gtake[:, :, :], FILLER))
                settle()
                for t in range(T):
                    for g in range(GROUPS):
                        link(nc.vector.max(best[:, t, g, :], sfc[:, t, g * GROUP:(g + 1) * GROUP]))
                settle()
                link(nc.vector.tensor_tensor(gscore[:, :, 0:GROUPS], best[:, :, :, 0], best[:, :, :, 1], ALU.add))
                settle()
                for t in range(T):
                    link(nc.vector.max(gbest[:, t, :], gscore[:, t, 0:GROUPS]))
                settle()
                link(nc.vector.tensor_copy(gtake[:, :, 0:TOPK_GROUP], gbest[:, :, 0:TOPK_GROUP]))
                settle()
                for t in range(T):
                    link(nc.vector.match_replace(gleft[:, t, :], gtake[:, t, :], gscore[:, t, :], PICKED))
                settle()
                link(nc.vector.tensor_scalar(gscore[:, :, 0:GROUPS], gleft[:, :, 0:GROUPS], PICKED, None, ALU.is_equal))
                settle()
                s4 = sfc[:, :, :].rearrange("p t (g e) -> p (t g) e", e=GROUP)
                for e in range(GROUP):
                    link(nc.vector.tensor_tensor(sfc[:, :, :].rearrange("p t (g e) -> p t g e", e=GROUP)[:, :, :, e],
                                                 sfc[:, :, :].rearrange("p t (g e) -> p t g e", e=GROUP)[:, :, :, e],
                                                 gscore[:, :, 0:GROUPS], ALU.mult))
                settle()
                link(nc.vector.tensor_scalar(sfc[:, :, :], sfc[:, :, :], 0.0, None, ALU.add))
                settle()
                for t in range(T):
                    link(nc.vector.max(gbest[:, t, :], sfc[:, t, :]))
                settle()
                for t in range(T):
                    link(nc.vector.match_replace(xn[:, t, 0:NE], gbest[:, t, :], sfc[:, t, :], PICKED))
                settle()
                link(nc.vector.tensor_scalar(sfc[:, :, :], xn[:, :, 0:NE], PICKED, None, ALU.is_equal))
                settle()
                link(nc.vector.tensor_tensor(sfc[:, :, :], sfc[:, :, :], scores[:, :, :], ALU.mult))
                settle()
                link(nc.vector.tensor_reduce(wsum[:, :], sfc[:, :, :], AX.X, ALU.add))
                settle()
                link(nc.vector.tensor_scalar(wsum[:, :], wsum[:, :], 1e-20, None, ALU.add))
                settle()
                link(nc.vector.reciprocal(wsum[:, :], wsum[:, :]))
                settle()
                for t in range(T):
                    s = t % 2
                    if t >= 2:
                        dve.wait_ge(coef_turned, t - 1)
                    link(nc.vector.tensor_scalar(coef[:, s, :], sfc[:, t, :], wsum[:, t:t + 1], ROUTE_SCALE,
                                                 ALU.mult, ALU.mult))
                    settle()
                    link(nc.vector.tensor_copy(crr[:, s, :], coef[:, s, :]))
                    settle()
                    link(nc.vector.tensor_copy(cr[:, s, 0, :], crr[:, s, :].bitcast(F32)))
                    nc.vector.tensor_tensor(cr[:, s, 1, :], coef[:, s, :], crr[:, s, :].bitcast(F32), ALU.subtract)\
                       .then_inc(coef_ready, 1)
                    settle()

        BG, BU, BC, BY, BYT = 0, 2, 4, 6, 7

        with nc.Block() as block:
            @block.tensor
            def _(pe):
                pe.sem_inc(unit_free, 1)
                with pe.Fori(0, NC) as c:
                    tok = bass.ds(c * CH, CH)

                    def down(k):
                        pe.wait_ge(h_done, ALLU * c + k + 1)
                        if k == 0:
                            pe.wait_ge(y_saved, c + 1)
                        last = nc.tensor.matmul(ps[:, BY, :], wd_sb[:, k, :], h[:, k % 2, :],
                                                start=(k == 0), stop=(k == ALLU - 1))
                        last.then_inc(down_done, 1)

                    for k in range(ALLU):
                        s, u = k % 2, ALLU * c + k
                        pe.wait_ge(unit_free, u + 1 if k == 0 else u)
                        for bank, w, done in ((BG, wgu[0], g_done), (BU, wgu[1], u_done)):
                            for n, (i, j) in enumerate(((0, 1), (1, 0), (0, 0))):
                                last = nc.tensor.matmul(ps[:, bank + s, :], w[:, i, k, :], xr[:, j, tok],
                                                        start=(n == 0), stop=(n == 2))
                            if done is u_done and k < UNITS:
                                last = nc.tensor.matmul(ps[:, BC + s, :], sel[:, k, :], coefT[:, tok],
                                                        start=True, stop=True)
                            last.then_inc(done, 1)
                        if k >= 1:
                            down(k - 1)
                    down(ALLU - 1)
                    pe.wait_ge(y_saved, c + 2)
                    for i in range(4):
                        last = nc.tensor.transpose(ps[:, BYT, i * P:(i + 1) * P], y_sb[:, i * P:(i + 1) * P], ident[:, :])
                    last.then_inc(y_turned, 1)

            @block.scalar
            def _(act):
                act.sem_inc(y_saved, 1)
                with act.Fori(0, NC) as c:
                    for k in range(ALLU):
                        s, u = k % 2, ALLU * c + k
                        act.wait_ge(g_done, u + 1)
                        act.wait_ge(unit_free, u + 1 if k == 0 else u)
                        nc.scalar.activation(gact[:, s, :], ps[:, BG + s, :], ACT.Silu).then_inc(act_done, 1)
                    act.wait_ge(down_done, ALLU * (c + 1))
                    nc.scalar.activation(y_sb[:, :], ps[:, BY, :], ACT.Copy).then_inc(y_saved, 1)

            @block.vector
            def _(dve):
                with dve.Fori(0, NC) as c:
                    for k in range(ALLU):
                        s, u = k % 2, ALLU * c + k
                        dve.wait_ge(act_done, u + 1)
                        dve.wait_ge(u_done, u + 1)
                        if k == 0:
                            dve.wait_ge(y_saved, c + 1)
                        elif k >= 2:
                            dve.wait_ge(down_done, u - 1)
                        if k < UNITS:
                            nc.vector.tensor_tensor(gu[:, s, :], ps[:, BU + s, :], gact[:, s, :], ALU.mult)\
                               .then_inc(gu_done, 1)
                            dve.wait_ge(gu_done, UNITS * c + k + 1)
                            nc.vector.tensor_tensor(h[:, s, :], ps[:, BC + s, :], gu[:, s, :], ALU.mult)\
                               .then_inc(h_done, 1)
                        else:
                            nc.vector.tensor_tensor(h[:, s, :], ps[:, BU + s, :], gact[:, s, :], ALU.mult)\
                               .then_inc(h_done, 1)
                        dve.wait_ge(h_done, u + 1)
                        dve.sem_inc(unit_free, 1)
                    dve.wait_ge(y_turned, c + 1)
                    dve.wait_ge(out_sent, 16 * QUAD * (c + 1))
                    nc.vector.scalar_tensor_tensor(
                        res[:, :], ps[:, BYT, :], tanh_g[:, 1:2],
                        x_sb[:, bass.ds(4 * c, 4), :].rearrange("p t d -> p (t d)"), ALU.mult, ALU.add)\
                       .then_inc(res_ready, 1)

            @block.sync
            def _(sp):
                sp.sem_inc(out_sent, 16 * QUAD)
                flat = v["out"].rearrange("b l d -> (b l) d")
                with sp.Fori(0, NC) as c:
                    sp.wait_ge(res_ready, c + 1)
                    for g in range(QUAD):
                        rows = flat[bass.ds(c * CH, CH), :].rearrange("(i g a) d -> i g a d", g=QUAD, a=P // E)
                        sp.dma_start(rows[:, g, :, :], res[:, g * D:(g + 1) * D]).then_inc(out_sent, 16)
                sp.wait_ge(out_sent, 16 * QUAD * (NC + 1))


def mix_turn(nc, pe, t, ps, attn, ident, attn_ready, attnT_ready, attn_turned):
    pe.wait_ge(attn_ready, 4 * (t // 4) + 4)
    if t >= 2:
        pe.wait_ge(attnT_ready, t - 1)
    nc.tensor.transpose(ps[:, 2 + t % 2, 0:P], attn[:, t // 4 % 2, t % 4, :], ident[:, :]).then_inc(attn_turned, 1)


def mix_project(nc, pe, t, ps, attnT, woT, attnT_ready, biased, projected):
    pe.wait_ge(attnT_ready, t + 1)
    if t >= 2:
        pe.wait_ge(biased, t - 1)
    nc.tensor.matmul(ps[:, 4 + t % 2, 0:P], attnT[:, t % 2, :], woT[:, :], start=True, stop=True).then_inc(projected, 1)


def finish_mix(nc, dve, t, v, ps, proj, projected, biased, mixed):
    dve.wait_ge(projected, t + 1)
    if t >= 2:
        dve.wait_ge(mixed, t - 1)
    nc.vector.tensor_tensor(proj[:, t % 2, :], ps[:, 4 + t % 2, 0:P], v["bo_b"][:, :], ALU.add).then_inc(biased, 1)
    dve.wait_ge(biased, t + 1)
    nc.vector.scalar_tensor_tensor(v["x_sb"][:, t, :], proj[:, t % 2, :], v["tanh_g"][:, 0:1], v["x_sb"][:, t, :],
                                   ALU.mult, ALU.add).then_inc(mixed, 1)


def router(nc, pe, c, ps, xnT, rwT, NE, xnT_ready, logits_ready):
    pe.wait_ge(xnT_ready, c + 1)
    for i in range(4):
        t = 4 * c + i
        k = 512 // NE
        last = nc.tensor.matmul(ps[:, 6 + t // k, (t % k) * NE:(t % k + 1) * NE], xnT[:, t * P:(t + 1) * P],
                                rwT[:, :], start=True, stop=True)
    last.then_inc(logits_ready, 1)


_INS = ['x', 'ctx_1024', 'g_xattn', 'g_ffn', 'L0_xattn_Wq', 'L0_xattn_bq', 'L0_xattn_Wo', 'L0_xattn_bo',
        'L0_ffn_router_w', 'L0_ffn_e_bias', 'L0_ffn_Wg', 'L0_ffn_Wu', 'L0_ffn_Wd', 'L0_ffn_SWg', 'L0_ffn_SWu',
        'L0_ffn_SWd']


def kernel(**inputs):
    import numpy as _np
    import concourse.bacc as _bacc
    from concourse import mybir as _mybir
    from concourse.bass_utils import run_bass_kernel_spmd as _run

    nc = _bacc.Bacc("TRN2", target_bir_lowering=False, num_devices=1)
    arrays, args = {}, []
    for name in _INS:
        a = _np.ascontiguousarray(inputs[name])
        arrays[f"in_{name}"] = a
        args.append(nc.dram_tensor(f"in_{name}", a.shape, _mybir.dt.from_np(a.dtype), kind="ExternalInput").ap())
    out = nc.dram_tensor("out_0", inputs['x'].shape, F32, kind="ExternalOutput").ap()
    build(nc, *args, out)
    r = _run(nc, [arrays], core_ids=[0])
    return r.results[0]["out_0"]
```

```python
from contextlib import ExitStack

import concourse.bass as bass
from concourse import mybir

F32 = mybir.dt.float32
F32R = mybir.dt.float32r
BF16 = mybir.dt.bfloat16
ALU = mybir.AluOpType
ACT = mybir.ActivationFunctionType
AX = mybir.AxisListType

P = 128
HEADS, E = 16, 8
QUAD = 4
EPS = 1e-5
ROUTE_SCALE = 2.5
TOPK_GROUP, TOPK, GROUPS = 4, 8, 8
PICKED = -3.0e38
FILLER = -1.0e38

SLOTS = [(0, 0, 0), (8, 0, 1), (16, 0, 2), (24, 1, 0), (40, 1, 1), (48, 2, 0)]
SHIFT_ROW, SHIFT_ROWS = 32, 2
SLOTS4 = 4
PROBS = 4


def build(nc, x, ctx, g_x, g_f, Wq, bq, Wo, bo, router_w, e_bias, Wg, Wu, Wd, SWg, SWu, SWd, out):
    B, L, D = x.shape
    S = ctx.shape[1]
    NE, _, I = Wg.shape
    T = B * L // P
    ST = -(-S // P)
    LAST = S - (ST - 1) * P
    CH = 4 * P
    SC = -(-S // CH)
    SPAD = ST * P
    NQ = B * HEADS // QUAD
    QPB = HEADS // QUAD
    SCALE = float(E) ** -0.5
    assert D == P and HEADS * E == P and L == 2 * P and QPB == SLOTS4 and ST % 2 == 1

    k_parts = nc.dram_tensor("k_parts", [3, B, P, SPAD], BF16).ap()
    q_parts = nc.dram_tensor("q_parts", [3, P, B * L], BF16).ap()

    with ExitStack() as top:
        def sb(name, shape, dt=F32, where=top):
            return where.enter_context(nc.sbuf_tensor(name, shape, dt))

        def sem(name):
            return top.enter_context(nc.semaphore(name))

        ps = top.enter_context(nc.psum_tensor("ps", [P, 8, CH], F32))
        ident = sb("ident", [P, P])
        wqT = sb("wqT", [P, P])
        woT = sb("woT", [P, P])
        rwT = sb("rwT", [P, NE])
        bo_b = sb("bo_b", [P, P])
        eb_b = sb("eb_b", [P, NE])
        gates = sb("gates", [P, 2])
        tanh_g = sb("tanh_g", [P, 2])
        stats = sb("stats", [P, T, 6])
        moments = sb("moments", [P, T, 2])
        rstd = sb("rstd", [P, T])
        o_sb = sb("o_sb", [P, NQ, L])

        UNITS = NE * I // P
        wg_sb = sb("wg_sb", [P, 2, UNITS + 1, P], F32R)
        sel = sb("sel", [P, UNITS, P], F32R)
        x_tiles = sb("x_tiles", [P, T, D])
        quad_loaded, ones_set = [sem(f"quad_loaded{i}") for i in range(SLOTS4)], sem("ones_set")
        x_loaded = sem("x_loaded")
        folded = lambda a: a.rearrange("(c two) (i g a) d -> c (two i) g a d", two=2, g=QUAD, a=P // E)

        v = dict(locals())
        with ExitStack() as held:
            v["v_sb"] = sb("v_sb", [P, B, ST, P], where=held)
            v["kst"] = sb("kst", [P, SLOTS4, 2, SPAD], BF16, where=held)
            v["qst"] = sb("qst", [P, SLOTS4, 2, 2 * L], BF16, where=held)
            project(nc, v)
            attend(nc, v)
        mix_and_experts(nc, v)


def load_slot_rows(sp, v, b, i, slot):
    kst, qst, L, S, quad_loaded = v["kst"], v["qst"], v["L"], v["S"], v["quad_loaded"]
    base, kp, qp = SLOTS[slot]
    for j in range(2):
        r = 64 * j + base
        kd = v["k_parts"][kp, bass.ds(b, 1), :, 0:S].rearrange("a p s -> (a p) s")
        kd = kd.rearrange("(h e) s -> e h s", e=E)[:, QUAD * i + j:QUAD * i + j + 3:2, :]
        sp.dma_start(kst[r:r + E, i, :, 0:S], kd).then_inc(quad_loaded[i], 16)
        qd = v["q_parts"][qp, :, bass.ds(b * L, L)]
        qd = qd.rearrange("(h e) l -> e h l", e=E)[:, QUAD * i + j:QUAD * i + j + 3:2, :]
        sp.dma_start(qst[r:r + E, i, :, j * L:(j + 1) * L], qd).then_inc(quad_loaded[i], 16)


def project(nc, v):
    top, sem = v["top"], v["sem"]
    ps, ident, wqT, woT, rwT = v["ps"], v["ident"], v["wqT"], v["woT"], v["rwT"]
    stats, moments, rstd = v["stats"], v["moments"], v["rstd"]
    B, L, D, S, T, ST, LAST, CH, SC = (v[n] for n in ("B", "L", "D", "S", "T", "ST", "LAST", "CH", "SC"))
    k_parts, q_parts, NE = v["k_parts"], v["q_parts"], v["NE"]

    v_sb = v["v_sb"]
    with ExitStack() as local:
        def sb(name, shape, dt=F32):
            return local.enter_context(nc.sbuf_tensor(name, shape, dt))

        w_raw = sb("w_raw", [P, 3, P])
        bq_col = sb("bq_col", [P, 1])
        bq_b = sb("bq_b", [P, P])
        room = v["o_sb"][:, :, :].rearrange("p q l -> p (q l)")
        xn = room[:, 0:T * D].rearrange("p (t d) -> p t d", d=D)
        raw = room[:, T * D:T * D + 16 * D].rearrange("p (n t d) -> p n t d", n=4, d=D)
        turned, full, rest = (room[:, at:at + 2 * CH].rearrange("p (s n) -> p s n", s=2)
                              for at in range(T * D + 16 * D, T * D + 16 * D + 6 * CH, 2 * CH))
        ones_row = room[0:SHIFT_ROWS, T * D + 16 * D + 6 * CH:T * D + 16 * D + 6 * CH + v["SPAD"] // 2].bitcast(BF16)
        x_sb = sb("x_sb", [P, T, D])
        NPART = 3
        parts = sb("parts", [P, NPART, 3, CH], BF16)

        loaded_small, loaded_x = sem("loaded_small"), sem("loaded_x")
        loaded_ctx = [sem(f"loaded_ctx{i}") for i in range(4)]
        parts_out = [sem(f"parts_out{i}") for i in range(NPART)]
        operands_zero, ones_set = sem("operands_zero"), v["ones_set"]
        ident_made, ident_ready = sem("ident_made"), sem("ident_ready")
        w_turned, w_ready = sem("w_turned"), sem("w_ready")
        stat_done, mean_done, var_ready, std_ready, rstd_ready, xn_ready = (
            sem(n) for n in ("stat_done", "mean_done", "var_ready", "std_ready", "rstd_ready", "xn_ready"))
        chunk_turned, chunk_ready = sem("chunk_turned"), sem("chunk_ready")
        k_done, k_saved, v_done, v_saved = sem("k_done"), sem("k_saved"), sem("v_done"), sem("v_saved")
        part1, rest1, part2, part3 = sem("part1"), sem("rest1"), sem("part2"), sem("part3")
        tanh_done = v["tanh_done"] = sem("tanh_done")

        chunks = [("k", b, c) for b in range(B) for c in range(SC)]
        chunks[SC:SC] = [("q", 0, c) for c in range(B * L // CH)]

        def tiles(kind, c):
            if kind == "q":
                return [(i, P) for i in range(4)]
            return [(t - 4 * c, LAST if t == ST - 1 else P) for t in range(4 * c, min(4 * c + 4, ST))]

        def width(kind, c):
            return sum(r for _, r in tiles(kind, c))

        ctx_count = {}
        seen = [0] * 4
        for n, (kind, b, c) in enumerate(chunks):
            if kind == "k":
                full_rows = sum(1 for _, r in tiles(kind, c) if r == P)
                partial = any(r < P for _, r in tiles(kind, c))
                seen[n % 4] += 16 * ((full_rows > 0) + partial)
                ctx_count[n] = seen[n % 4]

        FIRST_LOAD = SC + B * L // CH + 1
        assert FIRST_LOAD + 2 * len(SLOTS) <= len(chunks)

        def parts_leave(sp, n):
            kind, b, c = chunks[n]
            w = width(kind, c)
            to = k_parts[:, b, :, c * CH:c * CH + w] if kind == "k" else q_parts[:, :, c * CH:c * CH + w]
            sp.wait_ge(part3, n + 1)
            sp.dma_start(to.rearrange("t p s -> p t s"), parts[:, n % NPART, :, 0:w]).then_inc(parts_out[n % NPART], 16)

        with nc.Block() as block:
            @block.sync
            def _(sp):
                sp.dma_start(x_sb[:, :, :], v["x"].rearrange("b t_p d -> (b t_p) d").rearrange("(t p) d -> p t d", p=P))\
                  .then_inc(loaded_x, 16)
                for i, w in enumerate((v["Wq"], v["Wo"])):
                    sp.dma_start(w_raw[:, i, :], w).then_inc(loaded_small, 16)
                sp.dma_start(w_raw[0:NE, 2, :], v["router_w"]).then_inc(loaded_small, 16)
                sp.dma_start(bq_col[:, :], v["bq"].rearrange("(p a) -> p a", a=1)).then_inc(loaded_small, 16)
                row = lambda a: a.rearrange("(a n) -> a n", a=1)
                sp.dma_start(bq_b[:, :], row(v["bq"]).to_broadcast((P, P))).then_inc(loaded_small, 16)
                sp.dma_start(v["bo_b"][:, :], row(v["bo"]).to_broadcast((P, P))).then_inc(loaded_small, 16)
                sp.dma_start(v["eb_b"][:, :], row(v["e_bias"]).to_broadcast((P, NE))).then_inc(loaded_small, 16)
                sp.dma_start(v["gates"][:, 0:1], row(v["g_x"]).to_broadcast((P, 1))).then_inc(loaded_small, 16)
                sp.dma_start(v["gates"][:, 1:2], row(v["g_f"]).to_broadcast((P, 1))).then_inc(loaded_small, 16)

                def load_chunk(n):
                    kind, b, c = chunks[n]
                    if kind == "q":
                        return
                    if n >= 4:
                        sp.wait_ge(chunk_turned, n - 3)
                    whole = sum(1 for _, r in tiles(kind, c) if r == P)
                    first = c * CH
                    if whole:
                        sp.dma_start(raw[:, n % 4, 0:whole, :],
                                     v["ctx"][b, first:first + whole * P, :].rearrange("(t p) d -> p t d", p=P))\
                          .then_inc(loaded_ctx[n % 4], 16)
                    if whole < len(tiles(kind, c)):
                        sp.dma_start(raw[0:LAST, n % 4, whole, :], v["ctx"][b, first + whole * P:S, :])\
                          .then_inc(loaded_ctx[n % 4], 16)

                for n in range(4):
                    load_chunk(n)
                for n, (kind, b, c) in enumerate(chunks):
                    if n + 4 < len(chunks):
                        load_chunk(n + 4)
                    if n >= 1:
                        parts_leave(sp, n - 1)
                    if n == 4:
                        sp.wait_ge(operands_zero, 3)
                        for j in range(2):
                            r = 64 * j + SHIFT_ROW
                            ones = ones_row.rearrange("r (a s) -> r a s", a=1).to_broadcast(
                                (SHIFT_ROWS, 2 * SLOTS4, v["SPAD"]))
                            sp.dma_start(v["kst"][r:r + SHIFT_ROWS, :, :, :].rearrange("r i p s -> r (i p) s"), ones)\
                              .then_inc(ones_set, 16)
                    if n == FIRST_LOAD:
                        for s in range(NPART):
                            sp.wait_ge(parts_out[s], 16 * len(range(s, n, NPART)))
                        sp.wait_ge(ones_set, 32)
                    if FIRST_LOAD <= n < FIRST_LOAD + 2 * len(SLOTS):
                        load_slot_rows(sp, v, 0, (n - FIRST_LOAD) // len(SLOTS), (n - FIRST_LOAD) % len(SLOTS))
                parts_leave(sp, len(chunks) - 1)
                for s in range(NPART):
                    sp.wait_ge(parts_out[s], 16 * len(range(s, len(chunks), NPART)))

            @block.gpsimd
            def _(pool):
                nc.gpsimd.memset(ident[:, :], 0.0).then_inc(ident_made, 1)
                pool.wait_ge(ident_made, 1)
                nc.gpsimd.affine_select(out=ident[:, :], in_=ident[:, :], compare_op=ALU.not_equal, fill=1.0,
                                        base=0, pattern=[[-1, P]], channel_multiplier=1).then_inc(ident_ready, 1)
                for n, (kind, b, c) in enumerate(chunks):
                    w = width(kind, c)
                    pool.wait_ge(part2, n + 1)
                    nc.gpsimd.tensor_tensor(parts[:, n % NPART, 2, 0:w], rest[:, n % 2, 0:w],
                                            parts[:, n % NPART, 1, 0:w], ALU.subtract).then_inc(part3, 1)

            @block.tensor
            def _(pe):
                pe.wait_ge(ident_ready, 1)
                pe.wait_ge(loaded_small, 9 * 16)
                for i, n in enumerate((P, P, NE)):
                    last = nc.tensor.transpose(ps[:, 7, i * P:i * P + n], w_raw[0:n, i, :], ident[0:n, 0:n])
                last.then_inc(w_turned, 1)
                pe.wait_ge(w_ready, 1)

                def turn(n):
                    kind, b, c = chunks[n]
                    if kind == "k":
                        pe.wait_ge(loaded_ctx[n % 4], ctx_count[n])
                    else:
                        pe.wait_ge(xn_ready, T)
                    if n >= 2:
                        pe.wait_ge(chunk_ready, n - 1)
                    for i, r in tiles(kind, c):
                        src = raw[0:r, n % 4, i, :] if kind == "k" else xn[:, 4 * c + i, :]
                        last = nc.tensor.transpose(ps[:, n % 2, i * P:i * P + r], src, ident[0:r, 0:r])
                    last.then_inc(chunk_turned, 1)

                turn(0)
                values = 0
                for n, (kind, b, c) in enumerate(chunks):
                    if n + 1 < len(chunks):
                        turn(n + 1)
                    pe.wait_ge(chunk_ready, n + 1)
                    if n >= 2:
                        pe.wait_ge(k_saved, n - 1)
                    w = width(kind, c)
                    nc.tensor.matmul(ps[:, 2 + n % 2, 0:w], wqT[:, :], turned[:, n % 2, 0:w], start=True, stop=True)\
                      .then_inc(k_done, 1)
                    if kind == "k":
                        if values >= 1:
                            pe.wait_ge(v_saved, sum(1 for ch in chunks[:max(n - 1, 0)] if ch[0] == "k"))
                        for i, r in tiles(kind, c):
                            last = nc.tensor.matmul(ps[0:r, 4 + n % 2, i * P:(i + 1) * P],
                                                    turned[:, n % 2, i * P:i * P + r], wqT[:, :], start=True, stop=True)
                        last.then_inc(v_done, 1)
                        values += 1

            @block.scalar
            def _(act):
                act.wait_ge(w_turned, 1)
                for i, (dst, n) in enumerate(((wqT, P), (woT, P), (rwT, NE))):
                    last = nc.scalar.activation(dst[:, :], ps[:, 7, i * P:i * P + n], ACT.Copy)
                last.then_inc(w_ready, 1)

                def copy_turned(n):
                    w = width(chunks[n][0], chunks[n][2])
                    act.wait_ge(chunk_turned, n + 1)
                    if n >= 2:
                        act.wait_ge(k_done, n - 1)
                        vals = sum(1 for ch in chunks[:n - 1] if ch[0] == "k")
                        act.wait_ge(v_done, vals)
                    nc.scalar.activation(turned[:, n % 2, 0:w], ps[:, n % 2, 0:w], ACT.Copy).then_inc(chunk_ready, 1)

                def second(n):
                    w = width(chunks[n][0], chunks[n][2])
                    act.wait_ge(rest1, n + 1)
                    nc.scalar.activation(parts[:, n % NPART, 1, 0:w], rest[:, n % 2, 0:w], ACT.Copy).then_inc(part2, 1)

                copy_turned(0)
                act.wait_ge(var_ready, 1)
                nc.scalar.activation(rstd[:, :], rstd[:, :], ACT.Sqrt).then_inc(std_ready, 1)
                for n, (kind, b, c) in enumerate(chunks):
                    w, s = width(kind, c), n % 2
                    if n + 1 < len(chunks):
                        copy_turned(n + 1)
                    act.wait_ge(k_saved, n + 1)
                    if n >= NPART:
                        act.wait_ge(parts_out[n % NPART], 16 * (n // NPART))
                    nc.scalar.activation(parts[:, n % NPART, 0, 0:w], full[:, s, 0:w], ACT.Copy).then_inc(part1, 1)
                    if n >= 1:
                        second(n - 1)
                second(len(chunks) - 1)
                nc.scalar.activation(v["tanh_g"][:, :], v["gates"][:, :], ACT.Tanh).then_inc(tanh_done, 1)

            @block.vector
            def _(dve):
                dve.wait_ge(loaded_x, 16)
                for t in range(T):
                    nc.vector.bn_stats(stats[:, t, :], x_sb[:, t, :]).then_inc(stat_done, 1)
                for t in range(T):
                    dve.wait_ge(stat_done, t + 1)
                    nc.vector.bn_aggr(moments[:, t, :], stats[:, t, :]).then_inc(mean_done, 1)
                dve.wait_ge(mean_done, T)
                nc.vector.tensor_scalar(rstd[:, :], moments[:, :, 1], EPS, None, ALU.add).then_inc(var_ready, 1)
                nc.vector.memset(ones_row, 1.0).then_inc(operands_zero, 1)
                nc.vector.memset(v["kst"][:, :, :, :], 0.0).then_inc(operands_zero, 1)
                nc.vector.memset(v["qst"][:, :, :, :], 0.0).then_inc(operands_zero, 1)
                dve.wait_ge(loaded_small, 9 * 16)

                def first_rest(n):
                    w = width(chunks[n][0], chunks[n][2])
                    dve.wait_ge(part1, n + 1)
                    if n >= 2:
                        dve.wait_ge(part3, n - 1)
                    nc.vector.tensor_tensor(rest[:, n % 2, 0:w], full[:, n % 2, 0:w], parts[:, n % NPART, 0, 0:w],
                                            ALU.subtract).then_inc(rest1, 1)

                values = 0
                for n, (kind, b, c) in enumerate(chunks):
                    w, s = width(kind, c), n % 2
                    if n == 1:
                        dve.wait_ge(std_ready, 1)
                        nc.vector.reciprocal(rstd[:, :], rstd[:, :]).then_inc(rstd_ready, 1)
                        dve.wait_ge(rstd_ready, 1)
                        for t in range(T):
                            nc.vector.tensor_scalar(xn[:, t, :], x_sb[:, t, :], moments[:, t, 0:1], rstd[:, t:t + 1],
                                                    ALU.subtract, ALU.mult).then_inc(xn_ready, 1)
                    dve.wait_ge(k_done, n + 1)
                    if n >= 2:
                        dve.wait_ge(rest1, n - 1)
                    nc.vector.tensor_scalar(full[:, s, 0:w], ps[:, 2 + s, 0:w], bq_col[:, 0:1], None, ALU.add)\
                      .then_inc(k_saved, 1)
                    if kind == "k":
                        values += 1
                        dve.wait_ge(v_done, values)
                        whole = sum(1 for _, r in tiles(kind, c) if r == P)
                        if whole:
                            bias = bq_b[:, :].rearrange("p (a n) -> p a n", a=1).to_broadcast((P, whole, P))
                            last = nc.vector.tensor_tensor(
                                v_sb[:, b, 4 * c:4 * c + whole, :],
                                ps[:, 4 + s, 0:whole * P].rearrange("p (t n) -> p t n", n=P), bias, ALU.add)
                        if whole < len(tiles(kind, c)):
                            last = nc.vector.tensor_tensor(v_sb[0:LAST, b, ST - 1, :],
                                                           ps[0:LAST, 4 + s, whole * P:(whole + 1) * P],
                                                           bq_b[0:LAST, :], ALU.add)
                        last.then_inc(v_saved, 1)
                    if n >= 1:
                        first_rest(n - 1)
                first_rest(len(chunks) - 1)


def attend(nc, v):
    sem, ps, ident, o_sb, v_sb = v["sem"], v["ps"], v["ident"], v["o_sb"], v["v_sb"]
    B, L, S, ST, LAST, CH, SC, NQ, SCALE = (v[n] for n in ("B", "L", "S", "ST", "LAST", "CH", "SC", "NQ", "SCALE"))
    k_parts, q_parts, SPAD = v["k_parts"], v["q_parts"], v["SPAD"]
    LT = L // P
    MAXES = QUAD * LT * SC
    BM, NM, BO = 4, 3, 7
    TURN_AT = 3
    PLACE_AT = TURN_AT + 2
    TURN_CHUNKS = MAXES * (TURN_AT + 1) // ST
    BT = BM + TURN_CHUNKS % NM
    assert (MAXES + 1) % NM == 0

    def bank(k):
        return BM + (k + (k >= TURN_CHUNKS)) % NM
    LOADS = 2 * 2 * len(SLOTS) * 16

    with ExitStack() as local:
        def sb(name, shape, dt=F32):
            return local.enter_context(nc.sbuf_tensor(name, shape, dt))

        kst, qst = v["kst"], v["qst"]
        stage = sb("stage", [P, CH])
        probs = sb("probs", [P, PROBS, 2, 2 * L])
        vq = sb("vq", [P, 2, ST, QUAD, E + 1])
        mx = sb("mx", [P, 2, LT * QUAD, SC])
        negm = sb("negm", [P, LT * QUAD])
        negm1 = sb("negm1", [P, LT * QUAD], BF16)
        MP = 64 + SHIFT_ROW + SHIFT_ROWS
        mpad = sb("mpad", [P, LT, 2, P])

        quad_loaded, wg_sb, sel, UNITS, NE = v["quad_loaded"], v["wg_sb"], v["sel"], v["UNITS"], v["NE"]
        sel_zero, sel_made, sel_ready = sem("sel_zero"), sem("sel_made"), sem("sel_ready")
        ones_in_v, w_loaded, w_cut_hi, w_cut = sem("ones_in_v"), sem("w_loaded"), sem("w_cut_hi"), sem("w_cut")
        max_scored, max_free = sem("max_scored"), sem("max_free")
        max_taken, max_split, max_first = sem("max_taken"), sem("max_split"), sem("max_first")
        negmax_ready, negmax_turned, shift_placed = sem("negmax_ready"), sem("negmax_turned"), sem("shift_placed")
        shift_cleared, v_placed, v_settled = sem("shift_cleared"), sem("v_placed"), sem("v_settled")
        scores_ready, probs_ready, probs_free, out_free = (
            sem("scores_ready"), sem("probs_ready"), sem("probs_free"), sem("out_free"))

        def rows(t):
            return LAST if t == ST - 1 else P

        def chunk_list(t):
            return range(MAXES * t // ST, MAXES * (t + 1) // ST)

        with nc.Block() as block:
            @block.sync
            def _(sp):
                for i in range(2, SLOTS4):
                    for slot in range(len(SLOTS)):
                        load_slot_rows(sp, v, 0, i, slot)
                for c in range(v["T"] // QUAD):
                    for g in range(QUAD):
                        sp.dma_start(v["x_tiles"][:, QUAD * c + g, :], v["folded"](v["x"])[c, :, g, :, :])\
                          .then_inc(v["x_loaded"], 16)
                with sp.Fori(1, B) as b:
                    for i in range(SLOTS4):
                        sp.wait_ge(out_free, SLOTS4 * b + i - 1)
                        for slot in range(len(SLOTS)):
                            load_slot_rows(sp, v, b, i, slot)

            @block.gpsimd
            def _(pool):
                nc.gpsimd.memset(vq[:, :, :, :, :], 1.0).then_inc(ones_in_v, 1)

                def fetch_weights(units, src):
                    dst = stage[:, 0:units * P]
                    if units > 1:
                        dst = dst.rearrange("h (e i) -> h e i", i=v["I"])
                    pool.dma_start(dst, src).then_inc(w_loaded, 16)

                def cut_weights(first, units, done):
                    hi, lo = (wg_sb[:, part, bass.ds(first, units), :].rearrange("h u c -> h (u c)")
                              for part in range(2))
                    pool.wait_ge(w_loaded, 16 * (done + 1))
                    nc.gpsimd.tensor_copy(hi, stage[:, 0:units * P]).then_inc(w_cut_hi, 1)
                    pool.wait_ge(w_cut_hi, done + 1)
                    nc.gpsimd.tensor_tensor(lo, stage[:, 0:units * P], hi.bitcast(F32), ALU.subtract)\
                      .then_inc(w_cut, 1)

                fetch_weights(1, v["SWg"])
                cut_weights(UNITS, 1, 0)
                pool.wait_ge(ones_in_v, 1)
                with pool.Fori(0, B) as b:
                    for i in range(SLOTS4):
                        q = SLOTS4 * b + i
                        if i == 1:
                            pool.wait_ge(w_cut, b + 1)
                            fetch_weights(4, v["Wg"][bass.ds(8 * b, 8), :, :].rearrange("e h i -> h e i"))
                        pool.wait_ge(out_free, q + 1)
                        src = v_sb[:, bass.ds(b, 1), :, QUAD * E * i:QUAD * E * (i + 1)]\
                            .rearrange("p a t (g e) -> p (a t) g e", e=E)
                        nc.gpsimd.tensor_copy(vq[:, i % 2, 0:ST - 1, :, 0:E], src[:, 0:ST - 1, :, :])
                        nc.gpsimd.tensor_copy(vq[0:LAST, i % 2, ST - 1, :, 0:E], src[0:LAST, ST - 1, :, :])\
                          .then_inc(v_placed, 1)
                        pool.wait_ge(v_placed, q + 1)
                        pool.sem_inc(v_settled, 1)
                        for j in range(2):
                            r = 64 * j + SHIFT_ROW
                            nc.gpsimd.memset(qst[r:r + SHIFT_ROWS, (i + 2) % SLOTS4, :, :], 0.0)\
                              .then_inc(shift_cleared, 1)
                        pool.wait_ge(shift_cleared, 2 * q + 2)
                        if i == 2:
                            cut_weights(4 * b, 4, b + 1)
                pool.wait_ge(w_cut, B + 1)
                sel0 = stage[:, :].rearrange("p (u c) -> p u c", c=P)
                for n in range(UNITS // 4):
                    if n >= 1:
                        pool.wait_ge(sel_ready, n)
                    nc.gpsimd.memset(sel0[:, :, :], 0.0).then_inc(sel_zero, 1)
                    for half in range(2):
                        pool.wait_ge(sel_zero, n + 1)
                        if half:
                            pool.wait_ge(sel_made, 2 * n + 1)
                        rows_of = sel0[half * NE:(half + 1) * NE, :, :].rearrange("e u (a i) -> e u a i", a=2)
                        nc.gpsimd.affine_select(out=rows_of, in_=rows_of, compare_op=ALU.not_equal, fill=1.0,
                                                base=-8 * n, pattern=[[-2, 4], [-1, 2], [0, v["I"]]],
                                                channel_multiplier=1).then_inc(sel_made, 1)
                    pool.wait_ge(sel_made, 2 * n + 2)
                    nc.gpsimd.tensor_copy(sel[:, 4 * n:4 * n + 4, :], sel0[:, :, :]).then_inc(sel_ready, 1)

            @block.tensor
            def _(pe):
                def max_chunk(b, i, k):
                    c, g, lt = k % SC, (k // SC) % QUAD, k // (SC * QUAD)
                    p, j = g // 2, g % 2
                    w = min(CH, S - c * CH)
                    done = MAXES * (SLOTS4 * b + i) + k
                    place = k + (k >= TURN_CHUNKS) - NM
                    if place == TURN_CHUNKS and not (isinstance(b, int) and b == 0 and i == 0):
                        pe.wait_ge(shift_placed, 2 * (SLOTS4 * b + i - 1) + 2)
                    elif not (place < 0 and isinstance(b, int) and b == 0 and i == 0):
                        taken = place - (place > TURN_CHUNKS) if place >= 0 else place
                        pe.wait_ge(max_free, done - k + taken + 1)
                    nc.tensor.matmul(ps[:, bank(k), 0:w],
                                     qst[:, i, p, j * L + lt * P:j * L + (lt + 1) * P],
                                     kst[:, i, p, c * CH:c * CH + w], start=True, stop=True).then_inc(max_scored, 1)

                def turn_maxima(q, next_follows=True):
                    pe.wait_ge(negmax_ready, q + 1)
                    if next_follows:
                        pe.wait_ge(max_free, MAXES * (q + 1) + TURN_CHUNKS - NM + 1)
                    for p in range(2):
                        for lt in range(LT):
                            last = nc.tensor.transpose(ps[:, BT, p * L + lt * P:p * L + (lt + 1) * P],
                                                       mpad[:, lt, p, :], ident[:, :])
                    last.then_inc(negmax_turned, 1)

                def score(b, i, t, between):
                    n = ST * (SLOTS4 * b + i) + t
                    s = (i + t) % 2
                    if t == 0:
                        pe.wait_ge(shift_placed, 2 * (SLOTS4 * b + i) + 2)
                    if not (isinstance(n, int) and n < 2):
                        pe.wait_ge(probs_ready, n - 1)
                    m = rows(t)
                    for p in range(2):
                        last = nc.tensor.matmul(ps[0:m, 2 * s + p, :], kst[:, i, p, t * P:t * P + m],
                                                qst[:, i, p, :], start=True, stop=True)
                        if p == 0:
                            between()
                    last.then_inc(scores_ready, 1)

                def weigh(b, i, t, between):
                    q = SLOTS4 * b + i
                    n = ST * q + t
                    if t == 0:
                        pe.wait_ge(v_placed, q + 1)
                        pe.wait_ge(out_free, q + 2)
                    pe.wait_ge(probs_ready, n + 1)
                    m = rows(t)
                    for g in range(QUAD):
                        p, j = g // 2, g % 2
                        last = nc.tensor.matmul(ps[32 * g:32 * g + E + 1, BO, 0:L],
                                                vq[0:m, i % 2, t, g, :],
                                                probs[0:m, (i * ST + t) % PROBS, p, j * L:(j + 1) * L],
                                                start=(t == 0), stop=(t == ST - 1))
                        if g < QUAD - 1:
                            between(g)
                    last.then_inc(probs_free, 1)

                def batch(b, last_batch):
                    for i in range(SLOTS4):
                        for t in range(ST):
                            bm, im = (b, i + 2) if i + 2 < SLOTS4 else (b + 1, i + 2 - SLOTS4)
                            maxima = not (last_batch and i + 2 >= SLOTS4)
                            if maxima and t == 0:
                                pe.wait_ge(quad_loaded[im], LOADS * (bm + 1))
                                pe.wait_ge(shift_cleared, 2 * (SLOTS4 * b + i) + 2)
                            ks = iter(chunk_list(t) if maxima else ())

                            def next_chunk():
                                for k in ks:
                                    max_chunk(bm, im, k)
                                    break

                            i2, t2 = (i, t + 2) if t + 2 < ST else (i + 1, t + 2 - ST)
                            if i2 < SLOTS4:
                                score(b, i2, t2, lambda: None)
                            elif not last_batch:
                                score(b + 1, 0, t2, lambda: None)
                            next_chunk()
                            weigh(b, i, t, lambda g: next_chunk() if g in (0, 2) else None)
                            for k in ks:
                                max_chunk(bm, im, k)
                            if t == TURN_AT and not (last_batch and i + 1 >= SLOTS4):
                                turn_maxima(SLOTS4 * b + i + 1, not (last_batch and i + 2 >= SLOTS4))

                pe.sem_inc(probs_free, PROBS)
                for i in range(2):
                    pe.wait_ge(quad_loaded[i], LOADS)
                    for k in range(MAXES):
                        if i == 1 and k == TURN_CHUNKS:
                            turn_maxima(0)
                        max_chunk(0, i, k)
                score(0, 0, 0, lambda: None)
                score(0, 0, 1, lambda: None)
                with pe.Fori(0, B - 1) as b:
                    batch(b, False)
                batch(B - 1, True)

            @block.scalar
            def _(act):
                def place(q, i):
                    act.wait_ge(negmax_turned, q + 1)
                    for j in range(2):
                        r = 64 * j + SHIFT_ROW
                        nc.scalar.activation(qst[r:r + SHIFT_ROWS, i, :, j * L:(j + 1) * L],
                                             ps[r:r + SHIFT_ROWS, BT, :].rearrange("r (p l) -> r p l", p=2), ACT.Copy)\
                           .then_inc(shift_placed, 1)

                def batch(b, last_batch):
                    for i in range(SLOTS4):
                        for t in range(ST):
                            n = ST * (SLOTS4 * b + i) + t
                            m, s = rows(t), (i + t) % 2
                            act.wait_ge(scores_ready, n + 1)
                            act.wait_ge(probs_free, n + 1)
                            nc.scalar.activation(probs[0:m, (i * ST + t) % PROBS, :, :], ps[0:m, 2 * s:2 * s + 2, :],
                                                 ACT.Exp, scale=SCALE).then_inc(probs_ready, 1)
                            if t == PLACE_AT and not (last_batch and i + 1 >= SLOTS4):
                                place(SLOTS4 * b + i + 1, (i + 1) % SLOTS4)

                place(0, 0)
                with act.Fori(0, B - 1) as b:
                    batch(b, False)
                batch(B - 1, True)

            @block.vector
            def _(dve):
                nc.vector.memset(mpad[:, :, :, :], 0.0).then_inc(max_split, 1)
                nc.vector.memset(ps[:, BO, :], 0.0).then_inc(out_free, 2)
                maxpad = mpad[:, :, :, :].rearrange("m l p (j c) -> m (l p) j c", j=2)

                def take(b, i, k):
                    w = min(CH, S - (k % SC) * CH)
                    done = MAXES * (SLOTS4 * b + i) + k
                    dve.wait_ge(max_scored, done + 1)
                    nc.vector.reduce_max(mx[:, i % 2, k // SC, k % SC:k % SC + 1], ps[:, bank(k), 0:w], AX.X)\
                       .then_inc(max_free, 1)

                def negate(q, i, step):
                    one = negm1[:, :].rearrange("m (a j) -> m a j", j=2)
                    both = negm[:, :].rearrange("m (a j) -> m a j", j=2)
                    if step == 0:
                        dve.wait_ge(max_free, MAXES * (q + 1))
                        nc.vector.tensor_reduce(negm[:, :], mx[:, i % 2, :, :], AX.X, ALU.max, negate=True)\
                           .then_inc(max_taken, 1)
                    elif step == 1:
                        dve.wait_ge(max_taken, q + 1)
                        nc.vector.tensor_copy(negm1[:, :], negm[:, :]).then_inc(max_first, 1)
                    elif step == 2:
                        dve.wait_ge(max_first, q + 1)
                        if not (isinstance(q, int) and q < 1):
                            dve.wait_ge(negmax_turned, q)
                        nc.vector.tensor_copy(maxpad[:, :, :, SHIFT_ROW], one).then_inc(max_split, 1)
                    elif step == 3:
                        dve.wait_ge(max_split, q + 2)
                        nc.vector.tensor_tensor(maxpad[:, :, :, SHIFT_ROW + 1], both, one, ALU.subtract)\
                           .then_inc(negmax_ready, 1)

                def save(q):
                    dve.wait_ge(probs_free, PROBS + ST * (q + 1))
                    dst = o_sb[:, q:q + 1, :] if isinstance(q, int) else o_sb[:, bass.ds(q, 1), :]
                    nc.vector.tensor_copy(dst.rearrange("p a l -> p (a l)"), ps[:, BO, 0:L])\
                       .then_inc(out_free, 1)

                def batch(b, last_batch):
                    for i in range(SLOTS4):
                        q = SLOTS4 * b + i
                        maxima = not (last_batch and i + 2 >= SLOTS4)
                        bm, im = (b, i + 2) if i + 2 < SLOTS4 else (b + 1, i + 2 - SLOTS4)
                        for k in range(MAXES):
                            if maxima:
                                take(bm, im, k)
                            if not (last_batch and i + 1 >= SLOTS4):
                                negate(q + 1, i + 1, k)
                        save(q)

                for k in range(MAXES):
                    take(0, 0, k)
                for k in range(MAXES):
                    take(0, 1, k)
                    negate(0, 0, k)
                with dve.Fori(0, B - 1) as b:
                    batch(b, False)
                batch(B - 1, True)


def mix_and_experts(nc, v):
    sem, ps, ident, o_sb = v["sem"], v["ps"], v["ident"], v["o_sb"]
    B, L, D, T, CH, NE, I, QPB = (v[n] for n in ("B", "L", "D", "T", "CH", "NE", "I", "QPB"))
    stats, moments, rstd, tanh_g = v["stats"], v["moments"], v["rstd"], v["tanh_g"]
    woT, rwT, bo_b, eb_b = v["woT"], v["rwT"], v["bo_b"], v["eb_b"]
    LT = L // P
    UNITS = v["UNITS"]
    ALLU = UNITS + 1
    NC = B * L // CH
    GROUP = NE // GROUPS

    with ExitStack() as local:
        def sb(name, shape, dt=F32):
            return local.enter_context(nc.sbuf_tensor(name, shape, dt))

        den = sb("den", [P, 2, HEADS])
        attn = sb("attn", [P, 2, QUAD, P])
        attnT = sb("attnT", [P, 2, P])
        proj = sb("proj", [P, 2, P])
        room = o_sb[:, :, :].rearrange("p q l -> p (q l)")
        xn = room[:, 0:T * D].rearrange("p (t d) -> p t d", d=D)
        xnT = room[:, T * D:2 * T * D]
        xr = sb("xr", [P, 2, B * L], F32R)
        wd_sb = sb("wd_sb", [P, ALLU, D])
        wu_sb = sb("wu_sb", [P, 2, ALLU, P], F32R)
        wgu, sel = (v["wg_sb"], wu_sb), v["sel"]
        stage = sb("stage2", [P, 2, CH])
        x_sb = v["x_sb"] = v["x_tiles"]
        scores = sb("scores", [P, T, NE])
        sfc = sb("sfc", [P, T, NE])
        best = room[:, 2 * T * D:2 * T * D + T * GROUPS * 8].rearrange("p (t g k) -> p t g k", g=GROUPS, k=8)
        gscore = sb("gscore", [P, T, 2 * GROUPS])
        gbest = sb("gbest", [P, T, 8])
        gtake = sb("gtake", [P, T, 8])
        gleft = sb("gleft", [P, T, 2 * GROUPS])
        wsum = sb("wsum", [P, T])
        coef = sb("coef", [P, 2, NE])
        cr = sb("cr", [P, 2, 2, NE])
        crr = sb("crr", [P, 2, NE], F32R)
        coefT = sb("coefT", [P, B * L], F32R)
        gact = sb("gact", [P, 2, CH])
        gu = sb("gu", [P, 2, CH])
        h = sb("h", [P, 2, CH])
        y_sb = sb("y_sb", [P, CH])
        res = sb("res", [P, CH])

        turned_o, den_done, attn_ready, attn_turned, attnT_ready, projected = (
            sem(n) for n in ("turned_o", "den_done", "attn_ready", "attn_turned", "attnT_ready", "projected"))
        biased, mixed, stat2, mean2, var2, std2, rstd2, xn2_ready = (
            sem(n) for n in ("biased", "mixed", "stat2", "mean2", "var2", "std2", "rstd2", "xn2_ready"))
        xn_turned, xnT_ready, logits_ready, scores_done, xr_hi, xr_ready = (
            sem(n) for n in ("xn_turned", "xnT_ready", "logits_ready", "scores_done", "xr_hi", "xr_ready"))
        wd_loaded, wu_loaded, wu_cut_hi, wu_cut = (
            sem("wd_loaded"), [sem(f"wu_loaded{i}") for i in range(2)], sem("wu_cut_hi"), sem("wu_cut"))
        route, coef_ready, coef_turned, coefT_ready = (
            sem(n) for n in ("route", "coef_ready", "coef_turned", "coefT_ready"))
        g_done, act_done, u_done, gu_done, h_done, unit_free = (
            sem(n) for n in ("g_done", "act_done", "u_done", "gu_done", "h_done", "unit_free"))
        down_done, y_done, y_saved, y_turned, res_ready = (
            sem(n) for n in ("down_done", "y_done", "y_saved", "y_turned", "res_ready"))
        out_sent, x_loaded = sem("out_sent"), v["x_loaded"]

        queries = o_sb[:, :, :].rearrange("p q (a m) -> p q a m", m=P // E)

        with nc.Block() as block:
            @block.sync
            def _(sp):
                for n in range(UNITS // 4 + 1):
                    if n >= 2:
                        sp.wait_ge(wu_cut, n - 1)
                    if n < UNITS // 4:
                        sp.dma_start(stage[:, n % 2, :].rearrange("h (e i) -> h e i", i=I),
                                     v["Wu"][8 * n:8 * n + 8, :, :].rearrange("e h i -> h e i"))\
                          .then_inc(wu_loaded[n % 2], 16)
                    else:
                        sp.dma_start(stage[:, n % 2, 0:P], v["SWu"]).then_inc(wu_loaded[n % 2], 16)
            @block.gpsimd
            def _(pool):
                pool.dma_start(wd_sb[:, 0:UNITS, :], v["Wd"].rearrange("(u a) i h -> (a i) u h", a=2))\
                    .then_inc(wd_loaded, 16)
                pool.dma_start(wd_sb[:, UNITS, :], v["SWd"]).then_inc(wd_loaded, 16)
                for n in range(UNITS // 4 + 1):
                    units = 4 if n < UNITS // 4 else 1
                    hi, lo = (wu_sb[:, part, 4 * n:4 * n + units, :].rearrange("h u c -> h (u c)") for part in range(2))
                    pool.wait_ge(wu_loaded[n % 2], 16 * (n // 2 + 1))
                    nc.gpsimd.tensor_copy(hi, stage[:, n % 2, 0:units * P]).then_inc(wu_cut_hi, 1)
                    pool.wait_ge(wu_cut_hi, n + 1)
                    nc.gpsimd.tensor_tensor(lo, stage[:, n % 2, 0:units * P], hi.bitcast(F32), ALU.subtract)\
                      .then_inc(wu_cut, 1)
                pool.wait_ge(wd_loaded, 32)

            @block.tensor
            def _(pe):
                for t in range(T):
                    if t >= 2:
                        pe.wait_ge(attn_ready, t - 1)
                    for n in range(4):
                        m = t % 4 * 4 + n
                        last = nc.tensor.transpose(
                            ps[:, t % 2, n * P:(n + 1) * P],
                            queries[:, 8 * (t // 4):8 * (t // 4) + 8, :, m], ident[:, :])
                    last.then_inc(turned_o, 1)
                    if t % 4 == 3 and t > 4:
                        for u in range(t - 7, t - 3):
                            mix_turn(nc, pe, u, ps, attn, ident, attn_ready, attnT_ready, attn_turned)
                            if u >= 1:
                                mix_project(nc, pe, u - 1, ps, attnT, woT, attnT_ready, biased, projected)
                for u in range(T - 4, T):
                    mix_turn(nc, pe, u, ps, attn, ident, attn_ready, attnT_ready, attn_turned)
                    mix_project(nc, pe, u - 1, ps, attnT, woT, attnT_ready, biased, projected)
                mix_project(nc, pe, T - 1, ps, attnT, woT, attnT_ready, biased, projected)
                for c in range(NC):
                    pe.wait_ge(xn2_ready, 4 * c + 4)
                    if c >= 2:
                        pe.wait_ge(xnT_ready, c - 1)
                    for i in range(4):
                        last = nc.tensor.transpose(ps[:, c % 2, i * P:(i + 1) * P], xn[:, 4 * c + i, :], ident[:, :])
                    last.then_inc(xn_turned, 1)
                    if c >= 1:
                        router(nc, pe, c - 1, ps, xnT, rwT, NE, xnT_ready, logits_ready)
                router(nc, pe, NC - 1, ps, xnT, rwT, NE, xnT_ready, logits_ready)
                for t in range(T):
                    pe.wait_ge(coef_ready, t + 1)
                    if t >= 2:
                        pe.wait_ge(coefT_ready, t - 1)
                    nc.tensor.transpose(ps[:, t % 2, 0:P], cr[:, t % 2, :, :].rearrange("p a e -> p (a e)"), ident[:, :])\
                      .then_inc(coef_turned, 1)

            @block.scalar
            def _(act):
                for t in range(T):
                    act.wait_ge(attn_turned, t + 1)
                    if t >= 2:
                        act.wait_ge(projected, t - 1)
                    nc.scalar.activation(attnT[:, t % 2, :], ps[:, 2 + t % 2, 0:P], ACT.Copy).then_inc(attnT_ready, 1)
                act.wait_ge(var2, 1)
                nc.scalar.activation(rstd[:, :], rstd[:, :], ACT.Sqrt).then_inc(std2, 1)
                for c in range(NC):
                    act.wait_ge(xn_turned, c + 1)
                    nc.scalar.activation(xnT[:, c * CH:(c + 1) * CH], ps[:, c % 2, :], ACT.Copy).then_inc(xnT_ready, 1)
                for c in range(T * NE // CH):
                    act.wait_ge(logits_ready, (c + 1) * (CH // NE) // 4)
                    k = CH // NE
                    nc.scalar.activation(scores[:, k * c:k * (c + 1), :],
                                         ps[:, 6 + c, :].rearrange("p (t e) -> p t e", e=NE), ACT.Sigmoid)\
                      .then_inc(scores_done, 1)
                for t in range(T):
                    act.wait_ge(coef_turned, t + 1)
                    nc.scalar.activation(coefT[:, t * P:(t + 1) * P], ps[:, t % 2, 0:P], ACT.Copy)\
                      .then_inc(coefT_ready, 1)

            @block.vector
            def _(dve):
                dve.wait_ge(v["tanh_done"], 1)
                dve.wait_ge(x_loaded, 16 * T)
                for t in range(T):
                    o = ps[:, t % 2, :].rearrange("p (h c) -> p h c", c=32)
                    dve.wait_ge(turned_o, t + 1)
                    nc.vector.reciprocal(den[:, t % 2, :], o[:, :, E]).then_inc(den_done, 1)
                    dve.wait_ge(den_done, t + 1)
                    if t >= 8 and t % 4 == 0:
                        dve.wait_ge(attn_turned, t - 4)
                    d3 = den[:, t % 2, :].rearrange("p (h a) -> p h a", a=1).to_broadcast((P, HEADS, E))
                    at = attn[:, t // 4 % 2, :, t % 4 * 32:(t % 4 + 1) * 32].rearrange("p g (m e) -> p m g e", e=E)
                    nc.vector.tensor_tensor(at, o[:, :, 0:E].rearrange("p (m g) e -> p m g e", g=QUAD),
                                            d3.rearrange("p (m g) e -> p m g e", g=QUAD), ALU.mult)\
                       .then_inc(attn_ready, 1)
                    if t % 4 == 3 and t > 4:
                        for u in range(max(t - 8, 0), t - 4):
                            finish_mix(nc, dve, u, v, ps, proj, projected, biased, mixed)
                for u in range(T - 5, T):
                    finish_mix(nc, dve, u, v, ps, proj, projected, biased, mixed)
                for t in range(T):
                    dve.wait_ge(mixed, t + 1)
                    nc.vector.bn_stats(stats[:, t, :], x_sb[:, t, :]).then_inc(stat2, 1)
                for t in range(T):
                    dve.wait_ge(stat2, t + 1)
                    nc.vector.bn_aggr(moments[:, t, :], stats[:, t, :]).then_inc(mean2, 1)
                dve.wait_ge(mean2, T)
                nc.vector.tensor_scalar(rstd[:, :], moments[:, :, 1], EPS, None, ALU.add).then_inc(var2, 1)
                dve.wait_ge(std2, 1)
                nc.vector.reciprocal(rstd[:, :], rstd[:, :]).then_inc(rstd2, 1)
                dve.wait_ge(rstd2, 1)
                for t in range(T):
                    nc.vector.tensor_scalar(xn[:, t, :], x_sb[:, t, :], moments[:, t, 0:1], rstd[:, t:t + 1],
                                            ALU.subtract, ALU.mult).then_inc(xn2_ready, 1)
                for c in range(NC):
                    dve.wait_ge(xnT_ready, c + 1)
                    part = slice(c * CH, (c + 1) * CH)
                    nc.vector.tensor_copy(xr[:, 0, part], xnT[:, part]).then_inc(xr_hi, 1)
                    dve.wait_ge(xr_hi, c + 1)
                    nc.vector.tensor_tensor(xr[:, 1, part], xnT[:, part], xr[:, 0, part].bitcast(F32), ALU.subtract)\
                       .then_inc(xr_ready, 1)

                steps = [0]

                def link(ins):
                    steps[0] += 1
                    ins.then_inc(route, 1)

                def settle():
                    dve.wait_ge(route, steps[0])

                dve.wait_ge(scores_done, T * NE // CH)
                ebias = eb_b[:, :].rearrange("p (a e) -> p a e", a=1).to_broadcast((P, T, NE))
                link(nc.vector.tensor_tensor(sfc[:, :, :], scores[:, :, :], ebias, ALU.add))
                link(nc.vector.memset(gscore[:, :, :], FILLER))
                link(nc.vector.memset(gtake[:, :, :], FILLER))
                settle()
                for t in range(T):
                    for g in range(GROUPS):
                        link(nc.vector.max(best[:, t, g, :], sfc[:, t, g * GROUP:(g + 1) * GROUP]))
                settle()
                link(nc.vector.tensor_tensor(gscore[:, :, 0:GROUPS], best[:, :, :, 0], best[:, :, :, 1], ALU.add))
                settle()
                for t in range(T):
                    link(nc.vector.max(gbest[:, t, :], gscore[:, t, 0:GROUPS]))
                settle()
                link(nc.vector.tensor_copy(gtake[:, :, 0:TOPK_GROUP], gbest[:, :, 0:TOPK_GROUP]))
                settle()
                for t in range(T):
                    link(nc.vector.match_replace(gleft[:, t, :], gtake[:, t, :], gscore[:, t, :], PICKED))
                settle()
                link(nc.vector.tensor_scalar(gscore[:, :, 0:GROUPS], gleft[:, :, 0:GROUPS], PICKED, None, ALU.is_equal))
                settle()
                s4 = sfc[:, :, :].rearrange("p t (g e) -> p (t g) e", e=GROUP)
                for e in range(GROUP):
                    link(nc.vector.tensor_tensor(sfc[:, :, :].rearrange("p t (g e) -> p t g e", e=GROUP)[:, :, :, e],
                                                 sfc[:, :, :].rearrange("p t (g e) -> p t g e", e=GROUP)[:, :, :, e],
                                                 gscore[:, :, 0:GROUPS], ALU.mult))
                settle()
                link(nc.vector.tensor_scalar(sfc[:, :, :], sfc[:, :, :], 0.0, None, ALU.add))
                settle()
                for t in range(T):
                    link(nc.vector.max(gbest[:, t, :], sfc[:, t, :]))
                settle()
                for t in range(T):
                    link(nc.vector.match_replace(xn[:, t, 0:NE], gbest[:, t, :], sfc[:, t, :], PICKED))
                settle()
                link(nc.vector.tensor_scalar(sfc[:, :, :], xn[:, :, 0:NE], PICKED, None, ALU.is_equal))
                settle()
                link(nc.vector.tensor_tensor(sfc[:, :, :], sfc[:, :, :], scores[:, :, :], ALU.mult))
                settle()
                link(nc.vector.tensor_reduce(wsum[:, :], sfc[:, :, :], AX.X, ALU.add))
                settle()
                link(nc.vector.tensor_scalar(wsum[:, :], wsum[:, :], 1e-20, None, ALU.add))
                settle()
                link(nc.vector.reciprocal(wsum[:, :], wsum[:, :]))
                settle()
                for t in range(T):
                    s = t % 2
                    if t >= 2:
                        dve.wait_ge(coef_turned, t - 1)
                    link(nc.vector.tensor_scalar(coef[:, s, :], sfc[:, t, :], wsum[:, t:t + 1], ROUTE_SCALE,
                                                 ALU.mult, ALU.mult))
                    settle()
                    link(nc.vector.tensor_copy(crr[:, s, :], coef[:, s, :]))
                    settle()
                    link(nc.vector.tensor_copy(cr[:, s, 0, :], crr[:, s, :].bitcast(F32)))
                    nc.vector.tensor_tensor(cr[:, s, 1, :], coef[:, s, :], crr[:, s, :].bitcast(F32), ALU.subtract)\
                       .then_inc(coef_ready, 1)
                    settle()

        BG, BU, BC, BY, BYT = 0, 2, 4, 6, 7

        with nc.Block() as block:
            @block.tensor
            def _(pe):
                pe.sem_inc(unit_free, 1)
                with pe.Fori(0, NC) as c:
                    tok = bass.ds(c * CH, CH)

                    def down(k):
                        pe.wait_ge(h_done, ALLU * c + k + 1)
                        if k == 0:
                            pe.wait_ge(y_saved, c + 1)
                        last = nc.tensor.matmul(ps[:, BY, :], wd_sb[:, k, :], h[:, k % 2, :],
                                                start=(k == 0), stop=(k == ALLU - 1))
                        last.then_inc(down_done, 1)

                    for k in range(ALLU):
                        s, u = k % 2, ALLU * c + k
                        pe.wait_ge(unit_free, u + 1 if k == 0 else u)
                        for bank, w, done in ((BG, wgu[0], g_done), (BU, wgu[1], u_done)):
                            for n, (i, j) in enumerate(((0, 1), (1, 0), (0, 0))):
                                last = nc.tensor.matmul(ps[:, bank + s, :], w[:, i, k, :], xr[:, j, tok],
                                                        start=(n == 0), stop=(n == 2))
                            if done is u_done and k < UNITS:
                                last = nc.tensor.matmul(ps[:, BC + s, :], sel[:, k, :], coefT[:, tok],
                                                        start=True, stop=True)
                            last.then_inc(done, 1)
                        if k >= 1:
                            down(k - 1)
                    down(ALLU - 1)
                    pe.wait_ge(y_saved, c + 2)
                    for i in range(4):
                        last = nc.tensor.transpose(ps[:, BYT, i * P:(i + 1) * P], y_sb[:, i * P:(i + 1) * P], ident[:, :])
                    last.then_inc(y_turned, 1)

            @block.scalar
            def _(act):
                act.sem_inc(y_saved, 1)
                with act.Fori(0, NC) as c:
                    for k in range(ALLU):
                        s, u = k % 2, ALLU * c + k
                        act.wait_ge(g_done, u + 1)
                        act.wait_ge(unit_free, u + 1 if k == 0 else u)
                        nc.scalar.activation(gact[:, s, :], ps[:, BG + s, :], ACT.Silu).then_inc(act_done, 1)
                    act.wait_ge(down_done, ALLU * (c + 1))
                    nc.scalar.activation(y_sb[:, :], ps[:, BY, :], ACT.Copy).then_inc(y_saved, 1)

            @block.vector
            def _(dve):
                with dve.Fori(0, NC) as c:
                    for k in range(ALLU):
                        s, u = k % 2, ALLU * c + k
                        dve.wait_ge(act_done, u + 1)
                        dve.wait_ge(u_done, u + 1)
                        if k == 0:
                            dve.wait_ge(y_saved, c + 1)
                        elif k >= 2:
                            dve.wait_ge(down_done, u - 1)
                        if k < UNITS:
                            nc.vector.tensor_tensor(gu[:, s, :], ps[:, BU + s, :], gact[:, s, :], ALU.mult)\
                               .then_inc(gu_done, 1)
                            dve.wait_ge(gu_done, UNITS * c + k + 1)
                            nc.vector.tensor_tensor(h[:, s, :], ps[:, BC + s, :], gu[:, s, :], ALU.mult)\
                               .then_inc(h_done, 1)
                        else:
                            nc.vector.tensor_tensor(h[:, s, :], ps[:, BU + s, :], gact[:, s, :], ALU.mult)\
                               .then_inc(h_done, 1)
                        dve.wait_ge(h_done, u + 1)
                        dve.sem_inc(unit_free, 1)
                    dve.wait_ge(y_turned, c + 1)
                    dve.wait_ge(out_sent, 16 * QUAD * (c + 1))
                    nc.vector.scalar_tensor_tensor(
                        res[:, :], ps[:, BYT, :], tanh_g[:, 1:2],
                        x_sb[:, bass.ds(4 * c, 4), :].rearrange("p t d -> p (t d)"), ALU.mult, ALU.add)\
                       .then_inc(res_ready, 1)

            @block.sync
            def _(sp):
                sp.sem_inc(out_sent, 16 * QUAD)
                flat = v["out"].rearrange("b l d -> (b l) d")
                with sp.Fori(0, NC) as c:
                    sp.wait_ge(res_ready, c + 1)
                    for g in range(QUAD):
                        rows = flat[bass.ds(c * CH, CH), :].rearrange("(i g a) d -> i g a d", g=QUAD, a=P // E)
                        sp.dma_start(rows[:, g, :, :], res[:, g * D:(g + 1) * D]).then_inc(out_sent, 16)
                sp.wait_ge(out_sent, 16 * QUAD * (NC + 1))


def mix_turn(nc, pe, t, ps, attn, ident, attn_ready, attnT_ready, attn_turned):
    pe.wait_ge(attn_ready, 4 * (t // 4) + 4)
    if t >= 2:
        pe.wait_ge(attnT_ready, t - 1)
    nc.tensor.transpose(ps[:, 2 + t % 2, 0:P], attn[:, t // 4 % 2, t % 4, :], ident[:, :]).then_inc(attn_turned, 1)


def mix_project(nc, pe, t, ps, attnT, woT, attnT_ready, biased, projected):
    pe.wait_ge(attnT_ready, t + 1)
    if t >= 2:
        pe.wait_ge(biased, t - 1)
    nc.tensor.matmul(ps[:, 4 + t % 2, 0:P], attnT[:, t % 2, :], woT[:, :], start=True, stop=True).then_inc(projected, 1)


def finish_mix(nc, dve, t, v, ps, proj, projected, biased, mixed):
    dve.wait_ge(projected, t + 1)
    if t >= 2:
        dve.wait_ge(mixed, t - 1)
    nc.vector.tensor_tensor(proj[:, t % 2, :], ps[:, 4 + t % 2, 0:P], v["bo_b"][:, :], ALU.add).then_inc(biased, 1)
    dve.wait_ge(biased, t + 1)
    nc.vector.scalar_tensor_tensor(v["x_sb"][:, t, :], proj[:, t % 2, :], v["tanh_g"][:, 0:1], v["x_sb"][:, t, :],
                                   ALU.mult, ALU.add).then_inc(mixed, 1)


def router(nc, pe, c, ps, xnT, rwT, NE, xnT_ready, logits_ready):
    pe.wait_ge(xnT_ready, c + 1)
    for i in range(4):
        t = 4 * c + i
        k = 512 // NE
        last = nc.tensor.matmul(ps[:, 6 + t // k, (t % k) * NE:(t % k + 1) * NE], xnT[:, t * P:(t + 1) * P],
                                rwT[:, :], start=True, stop=True)
    last.then_inc(logits_ready, 1)


_INS = ['x', 'ctx_1024', 'g_xattn', 'g_ffn', 'L0_xattn_Wq', 'L0_xattn_bq', 'L0_xattn_Wo', 'L0_xattn_bo',
        'L0_ffn_router_w', 'L0_ffn_e_bias', 'L0_ffn_Wg', 'L0_ffn_Wu', 'L0_ffn_Wd', 'L0_ffn_SWg', 'L0_ffn_SWu',
        'L0_ffn_SWd']


def kernel(**inputs):
    import numpy as _np
    import concourse.bacc as _bacc
    from concourse import mybir as _mybir
    from concourse.bass_utils import run_bass_kernel_spmd as _run

    nc = _bacc.Bacc("TRN2", target_bir_lowering=False, num_devices=1)
    arrays, args = {}, []
    for name in _INS:
        a = _np.ascontiguousarray(inputs[name])
        arrays[f"in_{name}"] = a
        args.append(nc.dram_tensor(f"in_{name}", a.shape, _mybir.dt.from_np(a.dtype), kind="ExternalInput").ap())
    out = nc.dram_tensor("out_0", inputs['x'].shape, F32, kind="ExternalOutput").ap()
    build(nc, *args, out)
    r = _run(nc, [arrays], core_ids=[0])
    return r.results[0]["out_0"]
```

```python
from contextlib import ExitStack

import concourse.bass as bass
from concourse import mybir

F32 = mybir.dt.float32
F32R = mybir.dt.float32r
BF16 = mybir.dt.bfloat16
ALU = mybir.AluOpType
ACT = mybir.ActivationFunctionType
AX = mybir.AxisListType

P = 128
HEADS, E = 16, 8
QUAD = 4
EPS = 1e-5
ROUTE_SCALE = 2.5
TOPK_GROUP, TOPK, GROUPS = 4, 8, 8
PICKED = -3.0e38
FILLER = -1.0e38

SLOTS = [(0, 0, 0), (8, 0, 1), (16, 0, 2), (24, 1, 0), (40, 1, 1), (48, 2, 0)]
SHIFT_ROW, SHIFT_ROWS = 32, 2
SLOTS4 = 4
PROBS = 4


def build(nc, x, ctx, g_x, g_f, Wq, bq, Wo, bo, router_w, e_bias, Wg, Wu, Wd, SWg, SWu, SWd, out):
    B, L, D = x.shape
    S = ctx.shape[1]
    NE, _, I = Wg.shape
    T = B * L // P
    ST = -(-S // P)
    LAST = S - (ST - 1) * P
    CH = 4 * P
    SC = -(-S // CH)
    SPAD = ST * P
    NQ = B * HEADS // QUAD
    QPB = HEADS // QUAD
    SCALE = float(E) ** -0.5
    assert D == P and HEADS * E == P and L == 2 * P and QPB == SLOTS4 and ST % 2 == 1

    k_parts = nc.dram_tensor("k_parts", [3, B, P, SPAD], BF16).ap()
    q_parts = nc.dram_tensor("q_parts", [3, P, B * L], BF16).ap()

    with ExitStack() as top:
        def sb(name, shape, dt=F32, where=top):
            return where.enter_context(nc.sbuf_tensor(name, shape, dt))

        def sem(name):
            return top.enter_context(nc.semaphore(name))

        ps = top.enter_context(nc.psum_tensor("ps", [P, 8, CH], F32))
        ident = sb("ident", [P, P])
        wqT = sb("wqT", [P, P])
        woT = sb("woT", [P, P])
        rwT = sb("rwT", [P, NE])
        bo_b = sb("bo_b", [P, P])
        eb_b = sb("eb_b", [P, NE])
        gates = sb("gates", [P, 2])
        tanh_g = sb("tanh_g", [P, 2])
        stats = sb("stats", [P, T, 6])
        moments = sb("moments", [P, T, 2])
        rstd = sb("rstd", [P, T])
        o_sb = sb("o_sb", [P, NQ, L])

        UNITS = NE * I // P
        wg_sb = sb("wg_sb", [P, 2, UNITS + 1, P], F32R)
        sel = sb("sel", [P, UNITS, P], F32R)
        x_tiles = sb("x_tiles", [P, T, D])
        quad_loaded, ones_set = [sem(f"quad_loaded{i}") for i in range(SLOTS4)], sem("ones_set")
        x_loaded = sem("x_loaded")
        folded = lambda a: a.rearrange("(c two) (i g a) d -> c (two i) g a d", two=2, g=QUAD, a=P // E)

        v = dict(locals())
        with ExitStack() as held:
            v["v_sb"] = sb("v_sb", [P, B, ST, P], where=held)
            v["kst"] = sb("kst", [P, SLOTS4, 2, SPAD], BF16, where=held)
            v["qst"] = sb("qst", [P, SLOTS4, 2, 2 * L], BF16, where=held)
            project(nc, v)
            attend(nc, v)
        mix_and_experts(nc, v)


def load_slot_rows(sp, v, b, i, slot):
    kst, qst, L, S, quad_loaded = v["kst"], v["qst"], v["L"], v["S"], v["quad_loaded"]
    base, kp, qp = SLOTS[slot]
    for j in range(2):
        r = 64 * j + base
        kd = v["k_parts"][kp, bass.ds(b, 1), :, 0:S].rearrange("a p s -> (a p) s")
        kd = kd.rearrange("(h e) s -> e h s", e=E)[:, QUAD * i + j:QUAD * i + j + 3:2, :]
        sp.dma_start(kst[r:r + E, i, :, 0:S], kd).then_inc(quad_loaded[i], 16)
        qd = v["q_parts"][qp, :, bass.ds(b * L, L)]
        qd = qd.rearrange("(h e) l -> e h l", e=E)[:, QUAD * i + j:QUAD * i + j + 3:2, :]
        sp.dma_start(qst[r:r + E, i, :, j * L:(j + 1) * L], qd).then_inc(quad_loaded[i], 16)


def project(nc, v):
    top, sem = v["top"], v["sem"]
    ps, ident, wqT, woT, rwT = v["ps"], v["ident"], v["wqT"], v["woT"], v["rwT"]
    stats, moments, rstd = v["stats"], v["moments"], v["rstd"]
    B, L, D, S, T, ST, LAST, CH, SC = (v[n] for n in ("B", "L", "D", "S", "T", "ST", "LAST", "CH", "SC"))
    k_parts, q_parts, NE = v["k_parts"], v["q_parts"], v["NE"]

    v_sb = v["v_sb"]
    with ExitStack() as local:
        def sb(name, shape, dt=F32):
            return local.enter_context(nc.sbuf_tensor(name, shape, dt))

        w_raw = sb("w_raw", [P, 3, P])
        bq_col = sb("bq_col", [P, 1])
        bq_b = sb("bq_b", [P, P])
        room = v["o_sb"][:, :, :].rearrange("p q l -> p (q l)")
        xn = room[:, 0:T * D].rearrange("p (t d) -> p t d", d=D)
        RING = 8
        rings = (room[:, T * D:T * D + 16 * D].rearrange("p (n t d) -> p n t d", n=4, d=D),
                 v["x_tiles"][:, :, :].rearrange("p (n t) d -> p n t d", n=4))
        turned, full, rest = (room[:, at:at + 2 * CH].rearrange("p (s n) -> p s n", s=2)
                              for at in range(T * D + 16 * D, T * D + 16 * D + 6 * CH, 2 * CH))
        ones_row = room[0:SHIFT_ROWS, T * D + 16 * D + 6 * CH:T * D + 16 * D + 6 * CH + v["SPAD"] // 2].bitcast(BF16)
        x_sb = sb("x_sb", [P, T, D])
        NPART = 5
        parts = sb("parts", [P, NPART, 3, CH], BF16)

        loaded_w, loaded_bq, loaded_small, loaded_x = (
            sem("loaded_w"), sem("loaded_bq"), sem("loaded_small"), sem("loaded_x"))
        loaded_ctx = [sem(f"loaded_ctx{i}") for i in range(RING)]
        parts_out = [sem(f"parts_out{i}") for i in range(NPART)]
        operands_zero, ones_set = sem("operands_zero"), v["ones_set"]
        ident_made, ident_ready = sem("ident_made"), sem("ident_ready")
        w_turned, w_ready = sem("w_turned"), sem("w_ready")
        stat_done, mean_done, var_ready, std_ready, rstd_ready, xn_ready = (
            sem(n) for n in ("stat_done", "mean_done", "var_ready", "std_ready", "rstd_ready", "xn_ready"))
        chunk_turned, chunk_ready = sem("chunk_turned"), sem("chunk_ready")
        k_done, k_saved, v_done, v_saved = sem("k_done"), sem("k_saved"), sem("v_done"), sem("v_saved")
        part1, rest1, part2, part3 = sem("part1"), sem("rest1"), sem("part2"), sem("part3")
        tanh_done = v["tanh_done"] = sem("tanh_done")

        chunks = [("k", b, c) for b in range(B) for c in range(SC)]
        chunks[2 * SC:2 * SC] = [("q", 0, c) for c in range(B * L // CH)]

        def raw(n):
            return rings[n % RING // 4][:, n % 4]

        def tiles(kind, c):
            if kind == "q":
                return [(i, P) for i in range(4)]
            return [(t - 4 * c, LAST if t == ST - 1 else P) for t in range(4 * c, min(4 * c + 4, ST))]

        def width(kind, c):
            return sum(r for _, r in tiles(kind, c))

        ctx_count = {}
        seen = [0] * RING
        for n, (kind, b, c) in enumerate(chunks):
            if kind == "k":
                full_rows = sum(1 for _, r in tiles(kind, c) if r == P)
                partial = any(r < P for _, r in tiles(kind, c))
                seen[n % RING] += 16 * ((full_rows > 0) + partial)
                ctx_count[n] = seen[n % RING]

        STATS_AT = 1
        FIRST_LOAD = 2 * SC + B * L // CH + 1
        assert FIRST_LOAD + 2 * len(SLOTS) <= len(chunks)

        def parts_leave(sp, n):
            kind, b, c = chunks[n]
            w = width(kind, c)
            to = k_parts[:, b, :, c * CH:c * CH + w] if kind == "k" else q_parts[:, :, c * CH:c * CH + w]
            sp.wait_ge(part3, n + 1)
            sp.dma_start(to.rearrange("t p s -> p t s"), parts[:, n % NPART, :, 0:w]).then_inc(parts_out[n % NPART], 16)

        with nc.Block() as block:
            @block.sync
            def _(sp):
                def load_chunk(n):
                    kind, b, c = chunks[n]
                    if kind == "q":
                        return
                    if n >= RING:
                        sp.wait_ge(chunk_turned, n - RING + 1)
                    whole = sum(1 for _, r in tiles(kind, c) if r == P)
                    first = c * CH
                    if whole:
                        sp.dma_start(raw(n)[:, 0:whole, :],
                                     v["ctx"][b, first:first + whole * P, :].rearrange("(t p) d -> p t d", p=P))\
                          .then_inc(loaded_ctx[n % RING], 16)
                    if whole < len(tiles(kind, c)):
                        sp.dma_start(raw(n)[0:LAST, whole, :], v["ctx"][b, first + whole * P:S, :])\
                          .then_inc(loaded_ctx[n % RING], 16)

                AHEAD = RING - 2
                for i, w in enumerate((v["Wq"], v["Wo"])):
                    sp.dma_start(w_raw[:, i, :], w).then_inc(loaded_w, 16)
                sp.dma_start(w_raw[0:NE, 2, :], v["router_w"]).then_inc(loaded_w, 16)
                load_chunk(0)
                row = lambda a: a.rearrange("(a n) -> a n", a=1)
                sp.dma_start(bq_col[:, :], v["bq"].rearrange("(p a) -> p a", a=1)).then_inc(loaded_bq, 16)
                sp.dma_start(bq_b[:, :], row(v["bq"]).to_broadcast((P, P))).then_inc(loaded_bq, 16)
                load_chunk(1)
                sp.dma_start(x_sb[:, :, :], v["x"].rearrange("b t_p d -> (b t_p) d").rearrange("(t p) d -> p t d", p=P))\
                  .then_inc(loaded_x, 16)
                for n in range(2, AHEAD):
                    load_chunk(n)
                sp.dma_start(v["bo_b"][:, :], row(v["bo"]).to_broadcast((P, P))).then_inc(loaded_small, 16)
                sp.dma_start(v["eb_b"][:, :], row(v["e_bias"]).to_broadcast((P, NE))).then_inc(loaded_small, 16)
                sp.dma_start(v["gates"][:, 0:1], row(v["g_x"]).to_broadcast((P, 1))).then_inc(loaded_small, 16)
                sp.dma_start(v["gates"][:, 1:2], row(v["g_f"]).to_broadcast((P, 1))).then_inc(loaded_small, 16)
                for n, (kind, b, c) in enumerate(chunks):
                    if n + AHEAD < len(chunks):
                        load_chunk(n + AHEAD)
                    if n >= 1:
                        parts_leave(sp, n - 1)
                    if n == 4:
                        sp.wait_ge(operands_zero, 3)
                        for j in range(2):
                            r = 64 * j + SHIFT_ROW
                            ones = ones_row.rearrange("r (a s) -> r a s", a=1).to_broadcast(
                                (SHIFT_ROWS, 2 * SLOTS4, v["SPAD"]))
                            sp.dma_start(v["kst"][r:r + SHIFT_ROWS, :, :, :].rearrange("r i p s -> r (i p) s"), ones)\
                              .then_inc(ones_set, 16)
                    if n == FIRST_LOAD:
                        for s in range(NPART):
                            sp.wait_ge(parts_out[s], 16 * len(range(s, n, NPART)))
                        sp.wait_ge(ones_set, 32)
                    if FIRST_LOAD <= n < FIRST_LOAD + 2 * len(SLOTS):
                        load_slot_rows(sp, v, 0, (n - FIRST_LOAD) // len(SLOTS), (n - FIRST_LOAD) % len(SLOTS))
                parts_leave(sp, len(chunks) - 1)
                for s in range(NPART):
                    sp.wait_ge(parts_out[s], 16 * len(range(s, len(chunks), NPART)))

            @block.gpsimd
            def _(pool):
                nc.gpsimd.memset(ident[:, :], 0.0).then_inc(ident_made, 1)
                pool.wait_ge(ident_made, 1)
                nc.gpsimd.affine_select(out=ident[:, :], in_=ident[:, :], compare_op=ALU.not_equal, fill=1.0,
                                        base=0, pattern=[[-1, P]], channel_multiplier=1).then_inc(ident_ready, 1)

                nc.gpsimd.memset(v["kst"][:, :, :, :].rearrange("p i a s -> p (i a s)").bitcast(F32), 0.0)\
                  .then_inc(operands_zero, 1)
                nc.gpsimd.memset(v["qst"][:, :, :, :].rearrange("p i a s -> p (i a s)").bitcast(F32), 0.0)\
                  .then_inc(operands_zero, 1)
                nc.gpsimd.memset(ones_row, 1.0).then_inc(operands_zero, 1)
                for n, (kind, b, c) in enumerate(chunks):
                    w = width(kind, c)
                    pool.wait_ge(part2, n + 1)
                    nc.gpsimd.tensor_tensor(parts[:, n % NPART, 2, 0:w], rest[:, n % 2, 0:w],
                                            parts[:, n % NPART, 1, 0:w], ALU.subtract).then_inc(part3, 1)

            @block.tensor
            def _(pe):
                pe.wait_ge(ident_ready, 1)
                pe.wait_ge(loaded_w, 3 * 16)
                for i, n in enumerate((P, P, NE)):
                    last = nc.tensor.transpose(ps[:, 7, i * P:i * P + n], w_raw[0:n, i, :], ident[0:n, 0:n])
                last.then_inc(w_turned, 1)
                pe.wait_ge(w_ready, 1)

                def turn(n):
                    kind, b, c = chunks[n]
                    if kind == "k":
                        pe.wait_ge(loaded_ctx[n % RING], ctx_count[n])
                    else:
                        pe.wait_ge(xn_ready, T)
                    if n >= 2:
                        pe.wait_ge(chunk_ready, n - 1)
                    for i, r in tiles(kind, c):
                        src = raw(n)[0:r, i, :] if kind == "k" else xn[:, 4 * c + i, :]
                        last = nc.tensor.transpose(ps[:, n % 2, i * P:i * P + r], src, ident[0:r, 0:r])
                    last.then_inc(chunk_turned, 1)

                turn(0)
                values = 0
                for n, (kind, b, c) in enumerate(chunks):
                    if n + 1 < len(chunks):
                        turn(n + 1)
                    pe.wait_ge(chunk_ready, n + 1)
                    if n >= 2:
                        pe.wait_ge(k_saved, n - 1)
                    w = width(kind, c)
                    nc.tensor.matmul(ps[:, 2 + n % 2, 0:w], wqT[:, :], turned[:, n % 2, 0:w], start=True, stop=True)\
                      .then_inc(k_done, 1)
                    if kind == "k":
                        if values >= 1:
                            pe.wait_ge(v_saved, sum(1 for ch in chunks[:max(n - 1, 0)] if ch[0] == "k"))
                        for i, r in tiles(kind, c):
                            last = nc.tensor.matmul(ps[0:r, 4 + n % 2, i * P:(i + 1) * P],
                                                    turned[:, n % 2, i * P:i * P + r], wqT[:, :], start=True, stop=True)
                        last.then_inc(v_done, 1)
                        values += 1

            @block.scalar
            def _(act):
                act.wait_ge(w_turned, 1)
                for i, (dst, n) in enumerate(((wqT, P), (woT, P), (rwT, NE))):
                    last = nc.scalar.activation(dst[:, :], ps[:, 7, i * P:i * P + n], ACT.Copy)
                last.then_inc(w_ready, 1)

                def copy_turned(n):
                    w = width(chunks[n][0], chunks[n][2])
                    act.wait_ge(chunk_turned, n + 1)
                    if n >= 2:
                        act.wait_ge(k_done, n - 1)
                        vals = sum(1 for ch in chunks[:n - 1] if ch[0] == "k")
                        act.wait_ge(v_done, vals)
                    nc.scalar.activation(turned[:, n % 2, 0:w], ps[:, n % 2, 0:w], ACT.Copy).then_inc(chunk_ready, 1)

                def second(n):
                    w = width(chunks[n][0], chunks[n][2])
                    act.wait_ge(rest1, n + 1)
                    nc.scalar.activation(parts[:, n % NPART, 1, 0:w], rest[:, n % 2, 0:w], ACT.Copy).then_inc(part2, 1)

                copy_turned(0)
                copy_turned(1)
                for n, (kind, b, c) in enumerate(chunks):
                    w, s = width(kind, c), n % 2
                    act.wait_ge(k_saved, n + 1)
                    if n >= NPART:
                        act.wait_ge(parts_out[n % NPART], 16 * (n // NPART))
                    nc.scalar.activation(parts[:, n % NPART, 0, 0:w], full[:, s, 0:w], ACT.Copy).then_inc(part1, 1)
                    if n + 2 < len(chunks):
                        copy_turned(n + 2)
                    if n >= 1:
                        second(n - 1)
                    if n == STATS_AT:
                        act.wait_ge(var_ready, 1)
                        nc.scalar.activation(rstd[:, :], rstd[:, :], ACT.Sqrt).then_inc(std_ready, 1)
                second(len(chunks) - 1)
                act.wait_ge(loaded_small, 4 * 16)
                nc.scalar.activation(v["tanh_g"][:, :], v["gates"][:, :], ACT.Tanh).then_inc(tanh_done, 1)

            @block.vector
            def _(dve):
                dve.wait_ge(loaded_bq, 2 * 16)

                def first_rest(n):
                    w = width(chunks[n][0], chunks[n][2])
                    dve.wait_ge(part1, n + 1)
                    if n >= 2:
                        dve.wait_ge(part3, n - 1)
                    nc.vector.tensor_tensor(rest[:, n % 2, 0:w], full[:, n % 2, 0:w], parts[:, n % NPART, 0, 0:w],
                                            ALU.subtract).then_inc(rest1, 1)

                values = 0
                for n, (kind, b, c) in enumerate(chunks):
                    w, s = width(kind, c), n % 2
                    if n == STATS_AT:
                        dve.wait_ge(loaded_x, 16)
                        for t in range(T):
                            nc.vector.bn_stats(stats[:, t, :], x_sb[:, t, :]).then_inc(stat_done, 1)
                        for t in range(T):
                            dve.wait_ge(stat_done, t + 1)
                            nc.vector.bn_aggr(moments[:, t, :], stats[:, t, :]).then_inc(mean_done, 1)
                        dve.wait_ge(mean_done, T)
                        nc.vector.tensor_scalar(rstd[:, :], moments[:, :, 1], EPS, None, ALU.add).then_inc(var_ready, 1)
                    if n == STATS_AT + 2:
                        dve.wait_ge(std_ready, 1)
                        nc.vector.reciprocal(rstd[:, :], rstd[:, :]).then_inc(rstd_ready, 1)
                        dve.wait_ge(rstd_ready, 1)
                        for t in range(T):
                            nc.vector.tensor_scalar(xn[:, t, :], x_sb[:, t, :], moments[:, t, 0:1], rstd[:, t:t + 1],
                                                    ALU.subtract, ALU.mult).then_inc(xn_ready, 1)
                    dve.wait_ge(k_done, n + 1)
                    if n >= 2:
                        dve.wait_ge(rest1, n - 1)
                    nc.vector.tensor_scalar(full[:, s, 0:w], ps[:, 2 + s, 0:w], bq_col[:, 0:1], None, ALU.add)\
                      .then_inc(k_saved, 1)
                    if n >= 1:
                        first_rest(n - 1)
                    if kind == "k":
                        values += 1
                        dve.wait_ge(v_done, values)
                        whole = sum(1 for _, r in tiles(kind, c) if r == P)
                        if whole:
                            bias = bq_b[:, :].rearrange("p (a n) -> p a n", a=1).to_broadcast((P, whole, P))
                            last = nc.vector.tensor_tensor(
                                v_sb[:, b, 4 * c:4 * c + whole, :],
                                ps[:, 4 + s, 0:whole * P].rearrange("p (t n) -> p t n", n=P), bias, ALU.add)
                        if whole < len(tiles(kind, c)):
                            last = nc.vector.tensor_tensor(v_sb[0:LAST, b, ST - 1, :],
                                                           ps[0:LAST, 4 + s, whole * P:(whole + 1) * P],
                                                           bq_b[0:LAST, :], ALU.add)
                        last.then_inc(v_saved, 1)
                first_rest(len(chunks) - 1)


def attend(nc, v):
    sem, ps, ident, o_sb, v_sb = v["sem"], v["ps"], v["ident"], v["o_sb"], v["v_sb"]
    B, L, S, ST, LAST, CH, SC, NQ, SCALE = (v[n] for n in ("B", "L", "S", "ST", "LAST", "CH", "SC", "NQ", "SCALE"))
    k_parts, q_parts, SPAD = v["k_parts"], v["q_parts"], v["SPAD"]
    LT = L // P
    MAXES = QUAD * LT * SC
    BM, NM, BO = 4, 3, 7
    TURN_AT = 3
    PLACE_AT = TURN_AT + 2
    TURN_CHUNKS = MAXES * (TURN_AT + 1) // ST
    BT = BM + TURN_CHUNKS % NM
    assert (MAXES + 1) % NM == 0

    def bank(k):
        return BM + (k + (k >= TURN_CHUNKS)) % NM
    LOADS = 2 * 2 * len(SLOTS) * 16

    with ExitStack() as local:
        def sb(name, shape, dt=F32):
            return local.enter_context(nc.sbuf_tensor(name, shape, dt))

        kst, qst = v["kst"], v["qst"]
        stage = sb("stage", [P, CH])
        probs = sb("probs", [P, PROBS, 2, 2 * L])
        vq = sb("vq", [P, 2, ST, QUAD, E + 1])
        mx = sb("mx", [P, 2, LT * QUAD, SC])
        negm = sb("negm", [P, LT * QUAD])
        negm1 = sb("negm1", [P, LT * QUAD], BF16)
        MP = 64 + SHIFT_ROW + SHIFT_ROWS
        mpad = sb("mpad", [P, LT, 2, P])

        quad_loaded, wg_sb, UNITS = v["quad_loaded"], v["wg_sb"], v["UNITS"]
        bo_scaled = sem("bo_scaled")
        x_biased = v["x_biased"] = sem("x_biased")
        ones_in_v, w_loaded, w_cut_hi, w_cut = sem("ones_in_v"), sem("w_loaded"), sem("w_cut_hi"), sem("w_cut")
        max_scored, max_free = sem("max_scored"), sem("max_free")
        max_taken, max_split, max_first = sem("max_taken"), sem("max_split"), sem("max_first")
        negmax_ready, negmax_turned, shift_placed = sem("negmax_ready"), sem("negmax_turned"), sem("shift_placed")
        shift_cleared, v_placed, v_settled = sem("shift_cleared"), sem("v_placed"), sem("v_settled")
        scores_ready, probs_ready, probs_free, out_free = (
            sem("scores_ready"), sem("probs_ready"), sem("probs_free"), sem("out_free"))

        def rows(t):
            return LAST if t == ST - 1 else P

        def chunk_list(t):
            return range(MAXES * t // ST, MAXES * (t + 1) // ST)

        with nc.Block() as block:
            @block.sync
            def _(sp):
                for i in range(2, SLOTS4):
                    for slot in range(len(SLOTS)):
                        load_slot_rows(sp, v, 0, i, slot)
                for c in range(v["T"] // QUAD):
                    for g in range(QUAD):
                        sp.dma_start(v["x_tiles"][:, QUAD * c + g, :], v["folded"](v["x"])[c, :, g, :, :])\
                          .then_inc(v["x_loaded"], 16)
                with sp.Fori(1, B) as b:
                    for i in range(SLOTS4):
                        sp.wait_ge(out_free, SLOTS4 * b + i - 1)
                        for slot in range(len(SLOTS)):
                            load_slot_rows(sp, v, b, i, slot)

            @block.gpsimd
            def _(pool):
                nc.gpsimd.memset(vq[:, :, :, :, :], 1.0).then_inc(ones_in_v, 1)

                def fetch_weights(units, src):
                    dst = stage[:, 0:units * P]
                    if units > 1:
                        dst = dst.rearrange("h (e i) -> h e i", i=v["I"])
                    pool.dma_start(dst, src).then_inc(w_loaded, 16)

                def cut_weights(first, units, done):
                    hi, lo = (wg_sb[:, part, bass.ds(first, units), :].rearrange("h u c -> h (u c)")
                              for part in range(2))
                    pool.wait_ge(w_loaded, 16 * (done + 1))
                    nc.gpsimd.tensor_copy(hi, stage[:, 0:units * P]).then_inc(w_cut_hi, 1)
                    pool.wait_ge(w_cut_hi, done + 1)
                    nc.gpsimd.tensor_tensor(lo, stage[:, 0:units * P], hi.bitcast(F32), ALU.subtract)\
                      .then_inc(w_cut, 1)

                fetch_weights(1, v["SWg"])
                cut_weights(UNITS, 1, 0)
                pool.wait_ge(ones_in_v, 1)
                with pool.Fori(0, B) as b:
                    for i in range(SLOTS4):
                        q = SLOTS4 * b + i
                        if i == 1:
                            pool.wait_ge(w_cut, b + 1)
                            fetch_weights(4, v["Wg"][bass.ds(8 * b, 8), :, :].rearrange("e h i -> h e i"))
                        pool.wait_ge(out_free, q + 1)
                        src = v_sb[:, bass.ds(b, 1), :, QUAD * E * i:QUAD * E * (i + 1)]\
                            .rearrange("p a t (g e) -> p (a t) g e", e=E)
                        nc.gpsimd.tensor_copy(vq[:, i % 2, 0:ST - 1, :, 0:E], src[:, 0:ST - 1, :, :])
                        nc.gpsimd.tensor_copy(vq[0:LAST, i % 2, ST - 1, :, 0:E], src[0:LAST, ST - 1, :, :])\
                          .then_inc(v_placed, 1)
                        pool.wait_ge(v_placed, q + 1)
                        pool.sem_inc(v_settled, 1)
                        for j in range(2):
                            r = 64 * j + SHIFT_ROW
                            nc.gpsimd.memset(qst[r:r + SHIFT_ROWS, (i + 2) % SLOTS4, :, :], 0.0)\
                              .then_inc(shift_cleared, 1)
                        pool.wait_ge(shift_cleared, 2 * q + 2)
                        if i == 2:
                            cut_weights(4 * b, 4, b + 1)
                pool.wait_ge(bo_scaled, 1)
                pool.wait_ge(v["x_loaded"], 16 * v["T"])
                bias = v["bo_b"][:, :].rearrange("p (a d) -> p a d", a=1).to_broadcast((P, v["T"], P))
                nc.gpsimd.tensor_tensor(v["x_tiles"][:, :, :], v["x_tiles"][:, :, :], bias, ALU.add)\
                  .then_inc(x_biased, 1)

            @block.tensor
            def _(pe):
                def max_chunk(b, i, k):
                    c, g, lt = k % SC, (k // SC) % QUAD, k // (SC * QUAD)
                    p, j = g // 2, g % 2
                    w = min(CH, S - c * CH)
                    done = MAXES * (SLOTS4 * b + i) + k
                    place = k + (k >= TURN_CHUNKS) - NM
                    if place == TURN_CHUNKS and not (isinstance(b, int) and b == 0 and i == 0):
                        pe.wait_ge(shift_placed, 2 * (SLOTS4 * b + i - 1) + 2)
                    elif not (place < 0 and isinstance(b, int) and b == 0 and i == 0):
                        taken = place - (place > TURN_CHUNKS) if place >= 0 else place
                        pe.wait_ge(max_free, done - k + taken + 1)
                    nc.tensor.matmul(ps[:, bank(k), 0:w],
                                     qst[:, i, p, j * L + lt * P:j * L + (lt + 1) * P],
                                     kst[:, i, p, c * CH:c * CH + w], start=True, stop=True).then_inc(max_scored, 1)

                def turn_maxima(q, next_follows=True):
                    pe.wait_ge(negmax_ready, q + 1)
                    if next_follows:
                        pe.wait_ge(max_free, MAXES * (q + 1) + TURN_CHUNKS - NM + 1)
                    for p in range(2):
                        for lt in range(LT):
                            last = nc.tensor.transpose(ps[:, BT, p * L + lt * P:p * L + (lt + 1) * P],
                                                       mpad[:, lt, p, :], ident[:, :])
                    last.then_inc(negmax_turned, 1)

                def score(b, i, t, between):
                    n = ST * (SLOTS4 * b + i) + t
                    s = (i + t) % 2
                    if t == 0:
                        pe.wait_ge(shift_placed, 2 * (SLOTS4 * b + i) + 2)
                    if not (isinstance(n, int) and n < 2):
                        pe.wait_ge(probs_ready, n - 1)
                    m = rows(t)
                    for p in range(2):
                        last = nc.tensor.matmul(ps[0:m, 2 * s + p, :], kst[:, i, p, t * P:t * P + m],
                                                qst[:, i, p, :], start=True, stop=True)
                        if p == 0:
                            between()
                    last.then_inc(scores_ready, 1)

                def weigh(b, i, t, between):
                    q = SLOTS4 * b + i
                    n = ST * q + t
                    if t == 0:
                        pe.wait_ge(v_placed, q + 1)
                        pe.wait_ge(out_free, q + 2)
                    pe.wait_ge(probs_ready, n + 1)
                    m = rows(t)
                    for g in range(QUAD):
                        p, j = g // 2, g % 2
                        last = nc.tensor.matmul(ps[32 * g:32 * g + E + 1, BO, 0:L],
                                                vq[0:m, i % 2, t, g, :],
                                                probs[0:m, (i * ST + t) % PROBS, p, j * L:(j + 1) * L],
                                                start=(t == 0), stop=(t == ST - 1))
                        if g < QUAD - 1:
                            between(g)
                    last.then_inc(probs_free, 1)

                def batch(b, last_batch):
                    for i in range(SLOTS4):
                        for t in range(ST):
                            bm, im = (b, i + 2) if i + 2 < SLOTS4 else (b + 1, i + 2 - SLOTS4)
                            maxima = not (last_batch and i + 2 >= SLOTS4)
                            if maxima and t == 0:
                                pe.wait_ge(quad_loaded[im], LOADS * (bm + 1))
                                pe.wait_ge(shift_cleared, 2 * (SLOTS4 * b + i) + 2)
                            ks = iter(chunk_list(t) if maxima else ())

                            def next_chunk():
                                for k in ks:
                                    max_chunk(bm, im, k)
                                    break

                            i2, t2 = (i, t + 2) if t + 2 < ST else (i + 1, t + 2 - ST)
                            if i2 < SLOTS4:
                                score(b, i2, t2, lambda: None)
                            elif not last_batch:
                                score(b + 1, 0, t2, lambda: None)
                            next_chunk()
                            weigh(b, i, t, lambda g: next_chunk() if g in (0, 2) else None)
                            for k in ks:
                                max_chunk(bm, im, k)
                            if t == TURN_AT and not (last_batch and i + 1 >= SLOTS4):
                                turn_maxima(SLOTS4 * b + i + 1, not (last_batch and i + 2 >= SLOTS4))

                pe.sem_inc(probs_free, PROBS)
                for i in range(2):
                    pe.wait_ge(quad_loaded[i], LOADS)
                    for k in range(MAXES):
                        if i == 1 and k == TURN_CHUNKS:
                            turn_maxima(0)
                        max_chunk(0, i, k)
                score(0, 0, 0, lambda: None)
                score(0, 0, 1, lambda: None)
                with pe.Fori(0, B - 1) as b:
                    batch(b, False)
                batch(B - 1, True)

            @block.scalar
            def _(act):
                def place(q, i):
                    act.wait_ge(negmax_turned, q + 1)
                    for j in range(2):
                        r = 64 * j + SHIFT_ROW
                        nc.scalar.activation(qst[r:r + SHIFT_ROWS, i, :, j * L:(j + 1) * L],
                                             ps[r:r + SHIFT_ROWS, BT, :].rearrange("r (p l) -> r p l", p=2), ACT.Copy)\
                           .then_inc(shift_placed, 1)

                def batch(b, last_batch):
                    for i in range(SLOTS4):
                        for t in range(ST):
                            n = ST * (SLOTS4 * b + i) + t
                            m, s = rows(t), (i + t) % 2
                            act.wait_ge(scores_ready, n + 1)
                            act.wait_ge(probs_free, n + 1)
                            nc.scalar.activation(probs[0:m, (i * ST + t) % PROBS, :, :], ps[0:m, 2 * s:2 * s + 2, :],
                                                 ACT.Exp, scale=SCALE).then_inc(probs_ready, 1)
                            if t == PLACE_AT and not (last_batch and i + 1 >= SLOTS4):
                                place(SLOTS4 * b + i + 1, (i + 1) % SLOTS4)

                place(0, 0)
                with act.Fori(0, B - 1) as b:
                    batch(b, False)
                batch(B - 1, True)

            @block.vector
            def _(dve):
                nc.vector.memset(mpad[:, :, :, :], 0.0).then_inc(max_split, 1)
                nc.vector.memset(ps[:, BO, :], 0.0).then_inc(out_free, 2)
                dve.wait_ge(v["tanh_done"], 1)
                nc.vector.tensor_scalar(v["bo_b"][:, :], v["bo_b"][:, :], v["tanh_g"][:, 0:1], None, ALU.mult)\
                   .then_inc(bo_scaled, 1)
                maxpad = mpad[:, :, :, :].rearrange("m l p (j c) -> m (l p) j c", j=2)

                def take(b, i, k):
                    w = min(CH, S - (k % SC) * CH)
                    done = MAXES * (SLOTS4 * b + i) + k
                    dve.wait_ge(max_scored, done + 1)
                    nc.vector.reduce_max(mx[:, i % 2, k // SC, k % SC:k % SC + 1], ps[:, bank(k), 0:w], AX.X)\
                       .then_inc(max_free, 1)

                def negate(q, i, step):
                    one = negm1[:, :].rearrange("m (a j) -> m a j", j=2)
                    both = negm[:, :].rearrange("m (a j) -> m a j", j=2)
                    if step == 0:
                        dve.wait_ge(max_free, MAXES * (q + 1))
                        nc.vector.tensor_reduce(negm[:, :], mx[:, i % 2, :, :], AX.X, ALU.max, negate=True)\
                           .then_inc(max_taken, 1)
                    elif step == 1:
                        dve.wait_ge(max_taken, q + 1)
                        nc.vector.tensor_copy(negm1[:, :], negm[:, :]).then_inc(max_first, 1)
                    elif step == 2:
                        dve.wait_ge(max_first, q + 1)
                        if not (isinstance(q, int) and q < 1):
                            dve.wait_ge(negmax_turned, q)
                        nc.vector.tensor_copy(maxpad[:, :, :, SHIFT_ROW], one).then_inc(max_split, 1)
                    elif step == 3:
                        dve.wait_ge(max_split, q + 2)
                        nc.vector.tensor_tensor(maxpad[:, :, :, SHIFT_ROW + 1], both, one, ALU.subtract)\
                           .then_inc(negmax_ready, 1)

                def save(q):
                    dve.wait_ge(probs_free, PROBS + ST * (q + 1))
                    dst = o_sb[:, q:q + 1, :] if isinstance(q, int) else o_sb[:, bass.ds(q, 1), :]
                    nc.vector.tensor_copy(dst.rearrange("p a l -> p (a l)"), ps[:, BO, 0:L])\
                       .then_inc(out_free, 1)

                def batch(b, last_batch):
                    for i in range(SLOTS4):
                        q = SLOTS4 * b + i
                        maxima = not (last_batch and i + 2 >= SLOTS4)
                        bm, im = (b, i + 2) if i + 2 < SLOTS4 else (b + 1, i + 2 - SLOTS4)
                        for k in range(MAXES):
                            if maxima:
                                take(bm, im, k)
                            if not (last_batch and i + 1 >= SLOTS4):
                                negate(q + 1, i + 1, k)
                        save(q)

                for k in range(MAXES):
                    take(0, 0, k)
                for k in range(MAXES):
                    take(0, 1, k)
                    negate(0, 0, k)
                with dve.Fori(0, B - 1) as b:
                    batch(b, False)
                batch(B - 1, True)


def mix_and_experts(nc, v):
    sem, ps, ident, o_sb = v["sem"], v["ps"], v["ident"], v["o_sb"]
    B, L, D, T, CH, NE, I = (v[n] for n in ("B", "L", "D", "T", "CH", "NE", "I"))
    stats, moments, rstd, tanh_g = v["stats"], v["moments"], v["rstd"], v["tanh_g"]
    woT, rwT, eb_b, wgu_gate, sel = v["woT"], v["rwT"], v["eb_b"], v["wg_sb"], v["sel"]
    UNITS = v["UNITS"]
    ALLU = UNITS + 1
    NC = B * L // CH
    TPC = CH // P
    GROUP = NE // GROUPS
    STAGES = 4
    H3 = 3
    assert TPC == QUAD and ALLU % 2 == 1 and ALLU % H3 == 0 and 2 * NE == P and GROUP == 8 and T * NE == 2 * CH

    with ExitStack() as local:
        def sb(name, shape, dt=F32, where=local):
            return where.enter_context(nc.sbuf_tensor(name, shape, dt))

        xr = sb("xr", [P, 2, B * L], F32R)
        wu_sb = sb("wu_sb", [P, 2, ALLU, P], F32R)
        wd_sb = sb("wd_sb", [P, 2, ALLU, D], F32R)
        coefT = sb("coefT", [P, B * L], F32R)
        x_sb = v["x_tiles"]
        room = o_sb[:, :, :].rearrange("p q l -> p (q l)")
        taken = [0]

        def from_room(columns):
            taken[0] += columns
            assert taken[0] <= o_sb.shape[1] * o_sb.shape[2]
            return room[:, taken[0] - columns:taken[0]]

        scratch = from_room(T * D)
        xn = scratch.rearrange("p (t d) -> p t d", d=D)
        xnT = from_room(T * D)
        scores, sfc, coef = (from_room(T * NE).rearrange("p (t e) -> p t e", e=NE) for _ in range(3))
        gbest = from_room(T * 8).rearrange("p (t k) -> p t k", k=8)
        gtake = from_room(T * 8).rearrange("p (t k) -> p t k", k=8)
        gscore, gleft, gmask = (from_room(T * GROUPS).rearrange("p (t g) -> p t g", g=GROUPS) for _ in range(3))
        wsum = from_room(T)

        with ExitStack() as early:
            den = sb("den", [P, 2, 2 * HEADS], where=early)
            attn = sb("attn", [P, 2, QUAD, P], where=early)
            attnT = sb("attnT", [P, 2, CH], where=early)
            stage = sb("stage2", [P, STAGES, CH], where=early)
            cr = sb("cr", [P, T, 2, NE], F32R, where=early)
            ident2 = sb("ident2", [P, NE], where=early)

            turned_o, den_done, attn_ready, attn_turned, attnT_ready, projected = (
                sem(n) for n in ("turned_o", "den_done", "attn_ready", "attn_turned", "attnT_ready", "projected"))
            mixed, stat2, mean2, var2, std2, rstd2, xn2_ready = (
                sem(n) for n in ("mixed", "stat2", "mean2", "var2", "std2", "rstd2", "xn2_ready"))
            xn_turned, xnT_ready, logits_ready, scores_done, xr_hi, xr_ready = (
                sem(n) for n in ("xn_turned", "xnT_ready", "logits_ready", "scores_done", "xr_hi", "xr_ready"))
            w_arrived, w_high, w_parts = (
                [sem(f"w_arrived{i}") for i in range(STAGES)], sem("w_high"), sem("w_parts"))
            route, ident_folded, sel_ready, coef_done, coef_hi, coef_ready, coef_turned, coefT_ready = (
                sem(n) for n in ("route", "ident_folded", "sel_ready", "coef_done", "coef_hi", "coef_ready",
                                 "coef_turned", "coefT_ready"))

            queries = o_sb[:, :, :].rearrange("p q (a m) -> p q a m", m=P // E)

            cuts = []
            for n in range(UNITS // 4):
                cuts.append((v["Wu"][8 * n:8 * n + 8, :, :].rearrange("e h i -> h e i"), wu_sb, 4 * n, 4))
            cuts.append((v["SWu"], wu_sb, UNITS, 1))
            for n in range(UNITS // 4):
                cuts.append((v["Wd"][8 * n:8 * n + 8, :, :].rearrange("(u a) i h -> (a i) u h", a=2), wd_sb, 4 * n, 4))
            cuts.append((v["SWd"], wd_sb, UNITS, 1))

            def part_of(cut, part):
                _, w, first, units = cut
                return w[:, part, first:first + units, :].rearrange("h u c -> h (u c)")

            with nc.Block() as block:
                @block.sync
                def _(sp):
                    for n, (src, w, _, units) in enumerate(cuts):
                        if n >= STAGES:
                            sp.wait_ge(w_parts, n - STAGES + 1)
                        dst = stage[:, n % STAGES, 0:units * P]
                        if units > 1:
                            dst = dst.rearrange("h (e i) -> h e i", i=src.shape[2])
                        sp.dma_start(dst, src).then_inc(w_arrived[n % STAGES], 16)

                @block.gpsimd
                def _(pool):
                    nc.gpsimd.tensor_tensor(ident2[:, :], ident[:, 0:NE], ident[:, NE:2 * NE], ALU.add)\
                      .then_inc(ident_folded, 1)
                    for n, cut in enumerate(cuts):
                        if n == len(cuts) // 2:
                            for c in range(NC):
                                part = slice(c * CH, (c + 1) * CH)
                                pool.wait_ge(xr_hi, c + 1)
                                nc.gpsimd.tensor_tensor(xr[:, 1, part], xnT[:, part], xr[:, 0, part].bitcast(F32),
                                                        ALU.subtract).then_inc(xr_ready, 1)
                        pool.wait_ge(w_high, n + 1)
                        nc.gpsimd.tensor_tensor(part_of(cut, 1), stage[:, n % STAGES, 0:cut[3] * P],
                                                part_of(cut, 0).bitcast(F32), ALU.subtract).then_inc(w_parts, 1)

                @block.tensor
                def _(pe):
                    def turn_pair(r):
                        if r >= 2:
                            pe.wait_ge(attn_ready, r - 1)
                        for t in (2 * r, 2 * r + 1):
                            for n in range(4):
                                last = nc.tensor.transpose(
                                    ps[:, t % 4, n * P:(n + 1) * P],
                                    queries[:, 8 * (t // 4):8 * (t // 4) + 8, :, t % 4 * 4 + n], ident[:, :])
                        last.then_inc(turned_o, 1)

                    def turn_attn(c):
                        pe.wait_ge(attn_ready, 2 * c + 2)
                        if c >= 2:
                            pe.wait_ge(attnT_ready, c - 1)
                        for i in range(TPC):
                            last = nc.tensor.transpose(ps[:, 4 + c % 2, i * P:(i + 1) * P], attn[:, c % 2, i, :],
                                                       ident[:, :])
                        last.then_inc(attn_turned, 1)

                    def project_out(c):
                        pe.wait_ge(attnT_ready, c + 1)
                        if c >= 2:
                            pe.wait_ge(mixed, c - 1)
                        for i in range(TPC):
                            last = nc.tensor.matmul(ps[:, 6 + c % 2, i * P:(i + 1) * P],
                                                    attnT[:, c % 2, i * P:(i + 1) * P], woT[:, :],
                                                    start=True, stop=True)
                        last.then_inc(projected, 1)

                    def turn_xn(c):
                        pe.wait_ge(xn2_ready, c + 1)
                        if c >= 2:
                            pe.wait_ge(xr_hi, c - 1)
                        for i in range(TPC):
                            last = nc.tensor.transpose(ps[:, c % 2, i * P:(i + 1) * P], xn[:, TPC * c + i, :],
                                                       ident[:, :])
                        last.then_inc(xn_turned, 1)

                    def router(c):
                        pe.wait_ge(xnT_ready, c + 1)
                        k = CH // NE
                        for t in range(TPC * c, TPC * (c + 1)):
                            last = nc.tensor.matmul(ps[:, 2 + t // k, (t % k) * NE:(t % k + 1) * NE],
                                                    xnT[:, t * P:(t + 1) * P], rwT[:, :], start=True, stop=True)
                        last.then_inc(logits_ready, 1)

                    for c in range(NC):
                        turn_pair(2 * c)
                        turn_pair(2 * c + 1)
                        if c >= 2:
                            project_out(c - 2)
                        if c >= 1:
                            turn_attn(c - 1)
                    project_out(NC - 2)
                    turn_attn(NC - 1)
                    project_out(NC - 1)
                    for c in range(NC):
                        turn_xn(c)
                        if c >= 1:
                            router(c - 1)
                    router(NC - 1)
                    for c in range(NC):
                        pe.wait_ge(coef_ready, c + 1)
                        if c >= 2:
                            pe.wait_ge(coefT_ready, c - 1)
                        for i in range(TPC):
                            last = nc.tensor.transpose(
                                ps[:, c % 2, i * P:(i + 1) * P],
                                cr[:, TPC * c + i, :, :].rearrange("p a e -> p (a e)").bitcast(F32), ident[:, :])
                        last.then_inc(coef_turned, 1)

                @block.scalar
                def _(act):
                    def cut_high(n):
                        act.wait_ge(w_arrived[n % STAGES], 16 * (n // STAGES + 1))
                        nc.scalar.activation(part_of(cuts[n], 0), stage[:, n % STAGES, 0:cuts[n][3] * P], ACT.Copy)\
                          .then_inc(w_high, 1)

                    for c in range(NC):
                        act.wait_ge(attn_turned, c + 1)
                        if c >= 2:
                            act.wait_ge(projected, c - 1)
                        nc.scalar.activation(attnT[:, c % 2, :], ps[:, 4 + c % 2, :], ACT.Copy).then_inc(attnT_ready, 1)
                        cut_high(2 * c)
                        cut_high(2 * c + 1)
                    for c in range(NC):
                        act.wait_ge(var2, c + 1)
                        tiles = slice(TPC * c, TPC * (c + 1))
                        nc.scalar.activation(rstd[:, tiles], rstd[:, tiles], ACT.Sqrt).then_inc(std2, 1)
                    for c in range(NC):
                        act.wait_ge(xn_turned, c + 1)
                        part = slice(c * CH, (c + 1) * CH)
                        nc.scalar.activation(xnT[:, part], ps[:, c % 2, :], ACT.Copy).then_inc(xnT_ready, 1)
                        nc.scalar.activation(xr[:, 0, part], ps[:, c % 2, :], ACT.Copy).then_inc(xr_hi, 1)
                        cut_high(2 * NC + c)
                    k = CH // NE
                    for c in range(T // k):
                        act.wait_ge(logits_ready, (c + 1) * k // TPC)
                        nc.scalar.activation(scores[:, k * c:k * (c + 1), :],
                                             ps[:, 2 + c, :].rearrange("p (t e) -> p t e", e=NE), ACT.Sigmoid)\
                          .then_inc(scores_done, 1)
                    act.wait_ge(ident_folded, 1)
                    nc.scalar.activation(sel[:, :, :].rearrange("p u (a i) -> p (u a) i", a=2),
                                         ident2[:, :].rearrange("p (e a) -> p e a", a=1).to_broadcast((P, NE, I)),
                                         ACT.Copy).then_inc(sel_ready, 1)
                    for n in range(3 * NC, len(cuts)):
                        cut_high(n)
                    for c in range(NC):
                        tiles = slice(TPC * c, TPC * (c + 1))
                        act.wait_ge(coef_done, 1)
                        nc.scalar.activation(cr[:, tiles, 0, :], coef[:, tiles, :], ACT.Copy).then_inc(coef_hi, 1)
                    for c in range(NC):
                        act.wait_ge(coef_turned, c + 1)
                        nc.scalar.activation(coefT[:, c * CH:(c + 1) * CH], ps[:, c % 2, :], ACT.Copy)\
                          .then_inc(coefT_ready, 1)

                @block.vector
                def _(dve):
                    def normalise(r):
                        t = 2 * r
                        o = ps[:, t % 4:t % 4 + 2, :].rearrange("p b (h c) -> p (b h) c", c=32)
                        dve.wait_ge(turned_o, r + 1)
                        nc.vector.reciprocal(den[:, r % 2, :], o[:, :, E]).then_inc(den_done, 1)
                        dve.wait_ge(den_done, r + 1)
                        if r >= 4 and r % 2 == 0:
                            dve.wait_ge(attn_turned, r // 2 - 1)
                        d3 = den[:, r % 2, :].rearrange("p (h a) -> p h a", a=1).to_broadcast((P, 2 * HEADS, E))
                        at = attn[:, r // 2 % 2, :, r % 2 * 64:(r % 2 + 1) * 64].rearrange("p g (m e) -> p m g e", e=E)
                        nc.vector.tensor_tensor(at, o[:, :, 0:E].rearrange("p (m g) e -> p m g e", g=QUAD),
                                                d3.rearrange("p (m g) e -> p m g e", g=QUAD), ALU.mult)\
                           .then_inc(attn_ready, 1)

                    def mix(c):
                        tiles = x_sb[:, TPC * c:TPC * (c + 1), :].rearrange("p t d -> p (t d)")
                        dve.wait_ge(projected, c + 1)
                        nc.vector.scalar_tensor_tensor(tiles, ps[:, 6 + c % 2, :], tanh_g[:, 0:1], tiles,
                                                       ALU.mult, ALU.add).then_inc(mixed, 1)
                        dve.wait_ge(mixed, c + 1)
                        for t in range(TPC * c, TPC * (c + 1)):
                            nc.vector.bn_stats(stats[:, t, :], x_sb[:, t, :]).then_inc(stat2, 1)
                        for t in range(TPC * c, TPC * (c + 1)):
                            dve.wait_ge(stat2, t + 1)
                            nc.vector.bn_aggr(moments[:, t, :], stats[:, t, :]).then_inc(mean2, 1)
                        dve.wait_ge(mean2, TPC * (c + 1))
                        nc.vector.tensor_scalar(rstd[:, TPC * c:TPC * (c + 1)], moments[:, TPC * c:TPC * (c + 1), 1],
                                                EPS, None, ALU.add).then_inc(var2, 1)

                    def scale(c):
                        dve.wait_ge(std2, c + 1)
                        part = rstd[:, TPC * c:TPC * (c + 1)]
                        nc.vector.reciprocal(part, part).then_inc(rstd2, 1)
                        dve.wait_ge(rstd2, c + 1)
                        for t in range(TPC * c, TPC * (c + 1)):
                            last = nc.vector.tensor_scalar(xn[:, t, :], x_sb[:, t, :], moments[:, t, 0:1],
                                                           rstd[:, t:t + 1], ALU.subtract, ALU.mult)
                        last.then_inc(xn2_ready, 1)

                    dve.wait_ge(v["x_biased"], 1)
                    for r in range(6):
                        normalise(r)
                    mix(0)
                    normalise(6)
                    normalise(7)
                    mix(1)
                    scale(0)
                    mix(2)
                    scale(1)
                    mix(3)
                    scale(2)
                    scale(3)

                    steps = [0]

                    def link(ins):
                        steps[0] += 1
                        ins.then_inc(route, 1)

                    def settle():
                        dve.wait_ge(route, steps[0])

                    link(nc.vector.memset(gtake[:, :, :], FILLER))
                    half = T // 2
                    for n in range(2):
                        dve.wait_ge(scores_done, n + 1)
                        tiles = slice(half * n, half * (n + 1))
                        ebias = eb_b[:, :].rearrange("p (a e) -> p a e", a=1).to_broadcast((P, half, NE))
                        link(nc.vector.tensor_tensor(sfc[:, tiles, :], scores[:, tiles, :], ebias, ALU.add))
                    settle()
                    TG = T * GROUPS
                    pieces = [0]

                    def piece(width):
                        first = pieces[0] if pieces[0] + TG * width <= T * D else 0
                        pieces[0] = first + TG * width
                        return scratch[:, first:first + TG * width].rearrange("p (n w) -> p n w", w=width)

                    values = sfc[:, :, :].rearrange("p t (g e) -> p (t g) e", e=GROUP)
                    width = GROUP // 2
                    high, low = piece(width), piece(width)
                    link(nc.vector.tensor_tensor(high, values[:, :, 0:width], values[:, :, width:2 * width], ALU.max))
                    link(nc.vector.tensor_tensor(low, values[:, :, 0:width], values[:, :, width:2 * width], ALU.min))
                    settle()
                    while width > 1:
                        width //= 2
                        new_high, beaten, best_low, new_low = (piece(width) for _ in range(4))
                        a, b = slice(0, width), slice(width, 2 * width)
                        link(nc.vector.tensor_tensor(new_high, high[:, :, a], high[:, :, b], ALU.max))
                        link(nc.vector.tensor_tensor(beaten, high[:, :, a], high[:, :, b], ALU.min))
                        link(nc.vector.tensor_tensor(best_low, low[:, :, a], low[:, :, b], ALU.max))
                        settle()
                        link(nc.vector.tensor_tensor(new_low, beaten, best_low, ALU.max))
                        settle()
                        high, low = new_high, new_low
                    flat = lambda a: a.rearrange("p n w -> p (n w)")
                    link(nc.vector.tensor_tensor(gscore[:, :, :].rearrange("p t g -> p (t g)"), flat(high), flat(low),
                                                 ALU.add))
                    settle()
                    for t in range(T):
                        link(nc.vector.max(gbest[:, t, :], gscore[:, t, :]))
                    settle()
                    link(nc.vector.tensor_copy(gtake[:, :, 0:TOPK_GROUP], gbest[:, :, 0:TOPK_GROUP]))
                    settle()
                    for t in range(T):
                        link(nc.vector.match_replace(gleft[:, t, :], gtake[:, t, :], gscore[:, t, :], PICKED))
                    settle()
                    link(nc.vector.tensor_scalar(gmask[:, :, :], gleft[:, :, :], PICKED, None, ALU.is_equal))
                    settle()
                    gmasks = gmask[:, :, :].rearrange("p t (g a) -> p (t g) a", a=1).to_broadcast((P, TG, GROUP))
                    link(nc.vector.tensor_tensor(values, values, gmasks, ALU.mult))
                    settle()
                    link(nc.vector.tensor_scalar(sfc[:, :, :], sfc[:, :, :], 0.0, None, ALU.add))
                    settle()
                    for t in range(T):
                        link(nc.vector.max(gbest[:, t, :], sfc[:, t, :]))
                    settle()
                    left = scratch[:, 0:T * NE].rearrange("p (t e) -> p t e", e=NE)
                    for t in range(T):
                        link(nc.vector.match_replace(left[:, t, :], gbest[:, t, :], sfc[:, t, :], PICKED))
                    settle()
                    link(nc.vector.scalar_tensor_tensor(sfc[:, :, :], left, PICKED, scores[:, :, :],
                                                        ALU.is_equal, ALU.mult))
                    settle()
                    link(nc.vector.tensor_reduce(wsum[:, :], sfc[:, :, :], AX.X, ALU.add))
                    settle()
                    link(nc.vector.tensor_scalar(wsum[:, :], wsum[:, :], 1e-20, None, ALU.add))
                    settle()
                    link(nc.vector.reciprocal(wsum[:, :], wsum[:, :]))
                    settle()
                    wsums = wsum[:, :].rearrange("p (t a) -> p t a", a=1).to_broadcast((P, T, NE))
                    nc.vector.scalar_tensor_tensor(coef[:, :, :], sfc[:, :, :], ROUTE_SCALE, wsums,
                                                   ALU.mult, ALU.mult).then_inc(coef_done, 1)
                    for c in range(NC):
                        tiles = slice(TPC * c, TPC * (c + 1))
                        dve.wait_ge(coef_hi, c + 1)
                        nc.vector.tensor_tensor(cr[:, tiles, 1, :], coef[:, tiles, :], cr[:, tiles, 0, :].bitcast(F32),
                                                ALU.subtract).then_inc(coef_ready, 1)

        taken[0] = 0
        gact, h = (from_room(H3 * CH).rearrange("p (s c) -> p s c", c=CH) for _ in range(2))
        gu = from_room(2 * CH).rearrange("p (s c) -> p s c", c=CH)
        y_sb, res = from_room(CH), from_room(CH)
        hr = sb("hr", [P, 2, H3, CH], F32R)

        CREDIT = H3
        g_done, act_done, u_done, gu_done, h_done, h_high, h_cut = (
            sem(n) for n in ("g_done", "act_done", "u_done", "gu_done", "h_done", "h_high", "h_cut"))
        down_done, y_saved, y_turned, res_ready, out_sent = (
            sem(n) for n in ("down_done", "y_saved", "y_turned", "res_ready", "out_sent"))
        BG, BU, BC, BY, BYT = 0, 2, 4, 6, 7

        def gate_bank(k):
            return BYT if k == UNITS else BG + k % 2

        def up_bank(k):
            return BC if k == UNITS else BU + k % 2

        with nc.Block() as block:
            @block.tensor
            def _(pe):
                PASSES = ((0, 1), (1, 0), (0, 0))

                def gate_up(c, k):
                    u, tok = ALLU * c + k, bass.ds(c * CH, CH)
                    pe.wait_ge(h_done, CREDIT + (u - 1 if k >= 2 else u - 2))
                    for bank, w, done in ((gate_bank(k), wgu_gate, g_done), (up_bank(k), wu_sb, u_done)):
                        for n, (i, j) in enumerate(PASSES):
                            last = nc.tensor.matmul(ps[:, bank, :], w[:, i, k, :], xr[:, j, tok],
                                                    start=(n == 0), stop=(n == 2))
                        if done is u_done and k < UNITS:
                            if k == 0:
                                pe.wait_ge(h_done, CREDIT + u)
                            last = nc.tensor.matmul(ps[:, BC + k % 2, :], sel[:, k, :], coefT[:, tok],
                                                    start=True, stop=True)
                        last.then_inc(done, 1)

                def down(c, k):
                    pe.wait_ge(h_cut, CREDIT + ALLU * c + k + 1)
                    if k == 0:
                        pe.wait_ge(y_saved, c + 1)
                    for n, (i, j) in enumerate(PASSES):
                        last = nc.tensor.matmul(ps[:, BY, :], wd_sb[:, i, k, :], hr[:, j, k % H3, :],
                                                start=(k == 0 and n == 0), stop=(k == ALLU - 1 and n == 2))
                    last.then_inc(down_done, 1)

                def chunk(c, last_chunk):
                    for k in range(ALLU):
                        if k + 2 < ALLU:
                            gate_up(c, k + 2)
                        elif not last_chunk:
                            gate_up(c + 1, k + 2 - ALLU)
                        down(c, k)
                    pe.wait_ge(y_saved, c + 2)
                    for i in range(TPC):
                        last = nc.tensor.transpose(ps[:, BYT, i * P:(i + 1) * P], y_sb[:, i * P:(i + 1) * P],
                                                   ident[:, :])
                    last.then_inc(y_turned, 1)

                pe.sem_inc(down_done, CREDIT)
                gate_up(0, 0)
                gate_up(0, 1)
                with pe.Fori(0, NC - 1) as c:
                    chunk(c, False)
                chunk(NC - 1, True)

            @block.scalar
            def _(act):
                def gate(c, k):
                    u = ALLU * c + k
                    act.wait_ge(g_done, u + 1)
                    act.wait_ge(h_done, CREDIT + u - 2)
                    nc.scalar.activation(gact[:, k % H3, :], ps[:, gate_bank(k), :], ACT.Silu).then_inc(act_done, 1)

                def cut_high(c, k):
                    u = ALLU * c + k
                    act.wait_ge(h_done, CREDIT + u + 1)
                    act.wait_ge(down_done, CREDIT + u - 2)
                    nc.scalar.activation(hr[:, 0, k % H3, :], h[:, k % H3, :], ACT.Copy).then_inc(h_high, 1)

                def chunk(c, last_chunk):
                    for k in range(ALLU):
                        if k + 1 < ALLU:
                            gate(c, k + 1)
                        elif not last_chunk:
                            gate(c + 1, 0)
                        cut_high(c, k)
                    act.wait_ge(down_done, CREDIT + ALLU * (c + 1))
                    nc.scalar.activation(y_sb[:, :], ps[:, BY, :], ACT.Copy).then_inc(y_saved, 1)

                act.sem_inc(y_saved, 1)
                gate(0, 0)
                with act.Fori(0, NC - 1) as c:
                    chunk(c, False)
                chunk(NC - 1, True)

            @block.gpsimd
            def _(pool):
                pool.sem_inc(h_cut, CREDIT)
                with pool.Fori(0, NC) as c:
                    for k in range(ALLU):
                        pool.wait_ge(h_high, ALLU * c + k + 1)
                        nc.gpsimd.tensor_tensor(hr[:, 1, k % H3, :], h[:, k % H3, :],
                                                hr[:, 0, k % H3, :].bitcast(F32), ALU.subtract).then_inc(h_cut, 1)

            @block.vector
            def _(dve):
                def hidden(c, k):
                    s, u = k % 2, ALLU * c + k
                    dve.wait_ge(act_done, u + 1)
                    dve.wait_ge(u_done, u + 1)
                    dve.wait_ge(h_cut, CREDIT + u - 2)
                    if k < UNITS:
                        dve.wait_ge(h_done, CREDIT + (u - 1 if k else u - 2))
                        nc.vector.tensor_tensor(gu[:, s, :], ps[:, up_bank(k), :], gact[:, k % H3, :], ALU.mult)\
                           .then_inc(gu_done, 1)
                        dve.wait_ge(gu_done, UNITS * c + k + 1)
                        nc.vector.tensor_tensor(h[:, k % H3, :], ps[:, BC + s, :], gu[:, s, :], ALU.mult)\
                           .then_inc(h_done, 1)
                    else:
                        nc.vector.tensor_tensor(h[:, k % H3, :], ps[:, up_bank(k), :], gact[:, k % H3, :], ALU.mult)\
                           .then_inc(h_done, 1)

                def result(c):
                    dve.wait_ge(y_turned, c + 1)
                    dve.wait_ge(out_sent, 16 * QUAD * (c + 1))
                    tiles = x_sb[:, TPC * c:TPC * (c + 1), :] if isinstance(c, int) else x_sb[:, bass.ds(TPC * c, TPC), :]
                    nc.vector.scalar_tensor_tensor(res, ps[:, BYT, :], tanh_g[:, 1:2],
                                                   tiles.rearrange("p t d -> p (t d)"), ALU.mult, ALU.add)\
                       .then_inc(res_ready, 1)

                dve.sem_inc(h_done, CREDIT)
                hidden(0, 0)
                hidden(0, 1)
                with dve.Fori(0, NC - 1) as c:
                    for k in range(2, ALLU):
                        hidden(c, k)
                    hidden(c + 1, 0)
                    hidden(c + 1, 1)
                    result(c)
                for k in range(2, ALLU):
                    hidden(NC - 1, k)
                result(NC - 1)

            @block.sync
            def _(sp):
                sp.sem_inc(out_sent, 16 * QUAD)
                flat = v["out"].rearrange("b l d -> (b l) d")
                with sp.Fori(0, NC) as c:
                    sp.wait_ge(res_ready, c + 1)
                    for g in range(QUAD):
                        rows = flat[bass.ds(c * CH, CH), :].rearrange("(i g a) d -> i g a d", g=QUAD, a=P // E)
                        sp.dma_start(rows[:, g, :, :], res[:, g * D:(g + 1) * D]).then_inc(out_sent, 16)
                sp.wait_ge(out_sent, 16 * QUAD * (NC + 1))


_INS = ['x', 'ctx_1024', 'g_xattn', 'g_ffn', 'L0_xattn_Wq', 'L0_xattn_bq', 'L0_xattn_Wo', 'L0_xattn_bo',
        'L0_ffn_router_w', 'L0_ffn_e_bias', 'L0_ffn_Wg', 'L0_ffn_Wu', 'L0_ffn_Wd', 'L0_ffn_SWg', 'L0_ffn_SWu',
        'L0_ffn_SWd']


def kernel(**inputs):
    import numpy as _np
    import concourse.bacc as _bacc
    from concourse import mybir as _mybir
    from concourse.bass_utils import run_bass_kernel_spmd as _run

    nc = _bacc.Bacc("TRN2", target_bir_lowering=False, num_devices=1)
    arrays, args = {}, []
    for name in _INS:
        a = _np.ascontiguousarray(inputs[name])
        arrays[f"in_{name}"] = a
        args.append(nc.dram_tensor(f"in_{name}", a.shape, _mybir.dt.from_np(a.dtype), kind="ExternalInput").ap())
    out = nc.dram_tensor("out_0", inputs['x'].shape, F32, kind="ExternalOutput").ap()
    build(nc, *args, out)
    r = _run(nc, [arrays], core_ids=[0])
    return r.results[0]["out_0"]
```
